# Optimizing a Trainium2 kernel written in Bass

```python
import numpy as np
import jax
import jax.numpy as jnp

def _softmax(x, axis=-1):
    return jax.nn.softmax(x, axis=axis)

def _gelu(x):
    return jax.nn.gelu(x, approximate=True)

def _silu(x):
    return jax.nn.silu(x)

def _sigmoid(x):
    return jax.nn.sigmoid(x)

def _layernorm(x, axis=-1, eps=1e-05):
    m = jnp.mean(x, axis=axis, keepdims=True)
    v = jnp.var(x, axis=axis, keepdims=True)
    return (x - m) / jnp.sqrt(v + eps)

def _scatter_add(tgt, idx, src, axis=0):
    return tgt.at[idx].add(src)

def _segment_sum(src, seg, n):
    return jax.ops.segment_sum(src, seg, n)
kernel_name = 'mk_conv_seq_d2_conv_nchw512_r4_d43c47'

def setup_inputs(seed: int=0):
    np.random.seed(seed)
    _w = jnp.asarray

    def _rec_inputs():
        import jax
        import jax.numpy as jnp
        _gk = jax.random.key(seed)
        x = -0.0005153 + 1.001 * jax.random.normal(jax.random.fold_in(_gk, 1), (2, 128, 56, 56), jnp.float32)
        return x
    x = _rec_inputs()

    def _L0_conv_setup():
        import jax, jax.numpy as jnp
        import numpy as np
        N_HEAD, N_MIX, D_MODEL, D_K, D_V = (8, 2, 128, 16, 16)
        BN_EPS = 1e-05

        def avg_pool_3x3_s2(x):
            win = (1, 1, 3, 3)
            stride = (1, 1, 2, 2)
            pad = [(0, 0), (0, 0), (1, 1), (1, 1)]
            s = jax.lax.reduce_window(x, 0.0, jax.lax.add, win, stride, pad)
            ones = jnp.ones((1, 1, x.shape[2], x.shape[3]), x.dtype)
            cnt = jax.lax.reduce_window(ones, 0.0, jax.lax.add, win, stride, pad)
            return s / cnt

        def conv1x1(x, w, b=None):
            y = jnp.einsum('oc,bchw->bohw', w, x)
            if b is not None:
                y = y + b[None, :, None, None]
            return y
        key = jax.random.key(seed)
        ks = jax.random.split(key, 8)
        B, H, W = (2, 56, 56)
        std_kq = np.sqrt(2.0 / (D_MODEL + D_K)).astype(np.float32)
        std_v = np.sqrt(2.0 / (D_MODEL + D_V)).astype(np.float32)
        std_mix = np.power(N_MIX, -0.5).astype(np.float32)
        return {'x': jax.random.normal(ks[0], (B, D_MODEL, H, W), jnp.float32), 'w_qs': jax.random.normal(ks[1], (N_HEAD * D_K, D_MODEL), jnp.float32) * std_kq, 'b_qs': jnp.zeros((N_HEAD * D_K,), jnp.float32), 'w_vs': jax.random.normal(ks[2], (N_HEAD * D_V, D_MODEL), jnp.float32) * std_v, 'b_vs': jnp.zeros((N_HEAD * D_V,), jnp.float32), 'mix_w': jax.random.uniform(ks[3], (N_MIX, D_K), jnp.float32, -std_mix, std_mix), 'w_out': jax.random.normal(ks[4], (D_MODEL, N_HEAD * D_V), jnp.float32) * 0.02, 'bn_gamma': jnp.ones((D_MODEL,), jnp.float32), 'bn_beta': jnp.zeros((D_MODEL,), jnp.float32)}
    _L0_conv_all = _L0_conv_setup()
    _L0_conv_in = {k: v for k, v in _L0_conv_all.items() if k in ('w_qs', 'b_qs', 'w_vs', 'b_vs', 'mix_w', 'w_out', 'bn_gamma', 'bn_beta')}
    del _L0_conv_all

    def _L1_conv_setup():
        import jax, jax.numpy as jnp
        import numpy as np
        ALPHA = 32.0 ** 2
        HEADS = 8
        DIM_HEAD = 16
        EPS = 1e-05

        def _leaky(x):
            return jnp.where(x >= 0, x, 0.1 * x)

        def _cpb_bias(fmap_size, w0, b0, w1, b1, w2, b2):
            pos = jnp.arange(fmap_size)
            gi, gj = jnp.meshgrid(pos, pos, indexing='ij')
            grid = jnp.stack([gi, gj], axis=-1).reshape(-1, 2)
            rel = grid[:, None, :] - grid[None, :, :]
            rel = jnp.sign(rel) * jnp.log(jnp.abs(rel) + 1.0)
            h = _leaky(jnp.einsum('ijc,dc->ijd', rel.astype(jnp.float32), w0) + b0)
            h = _leaky(jnp.einsum('ijc,dc->ijd', h, w1) + b1)
            h = jnp.einsum('ijc,hc->ijh', h, w2) + b2
            return jnp.transpose(h, (2, 0, 1))

        def _stable_softmax(t, alpha=ALPHA):
            t = t / alpha
            t = t - jax.lax.stop_gradient(jnp.max(t, axis=-1, keepdims=True))
            return jax.nn.softmax(t * alpha, axis=-1)
        key = jax.random.key(seed)
        ks = jax.random.split(key, 9)
        B, C, H, W = (8, 128, 32, 32)
        inner = HEADS * DIM_HEAD
        s = 0.05
        return {'x': jax.random.normal(ks[0], (B, C, H, W), jnp.float32), 'gamma': jnp.ones((1, C, 1, 1), jnp.float32), 'w_qkv': jax.random.normal(ks[1], (inner * 3, C), jnp.float32) * s, 'w_out': jax.random.normal(ks[2], (C, inner), jnp.float32) * s, 'cpb_w0': jax.random.normal(ks[3], (32, 2), jnp.float32) * s, 'cpb_b0': jax.random.normal(ks[4], (32,), jnp.float32) * s, 'cpb_w1': jax.random.normal(ks[5], (32, 32), jnp.float32) * s, 'cpb_b1': jax.random.normal(ks[6], (32,), jnp.float32) * s, 'cpb_w2': jax.random.normal(ks[7], (HEADS, 32), jnp.float32) * s, 'cpb_b2': jax.random.normal(ks[8], (HEADS,), jnp.float32) * s}
    _L1_conv_all = _L1_conv_setup()
    _L1_conv_in = {k: v for k, v in _L1_conv_all.items() if k in ('gamma', 'w_qkv', 'w_out', 'cpb_w0', 'cpb_b0', 'cpb_w1', 'cpb_b1', 'cpb_w2', 'cpb_b2')}
    del _L1_conv_all
    return {'x': x, 'L0_conv_w_qs': _L0_conv_in['w_qs'], 'L0_conv_b_qs': _L0_conv_in['b_qs'], 'L0_conv_w_vs': _L0_conv_in['w_vs'], 'L0_conv_b_vs': _L0_conv_in['b_vs'], 'L0_conv_mix_w': _L0_conv_in['mix_w'], 'L0_conv_w_out': _L0_conv_in['w_out'], 'L0_conv_bn_gamma': _L0_conv_in['bn_gamma'], 'L0_conv_bn_beta': _L0_conv_in['bn_beta'], 'L1_conv_gamma': _L1_conv_in['gamma'], 'L1_conv_w_qkv': _L1_conv_in['w_qkv'], 'L1_conv_w_out': _L1_conv_in['w_out'], 'L1_conv_cpb_w0': _L1_conv_in['cpb_w0'], 'L1_conv_cpb_b0': _L1_conv_in['cpb_b0'], 'L1_conv_cpb_w1': _L1_conv_in['cpb_w1'], 'L1_conv_cpb_b1': _L1_conv_in['cpb_b1'], 'L1_conv_cpb_w2': _L1_conv_in['cpb_w2'], 'L1_conv_cpb_b2': _L1_conv_in['cpb_b2']}

def reference(x, L0_conv_w_qs, L0_conv_b_qs, L0_conv_w_vs, L0_conv_b_vs, L0_conv_mix_w, L0_conv_w_out, L0_conv_bn_gamma, L0_conv_bn_beta, L1_conv_gamma, L1_conv_w_qkv, L1_conv_w_out, L1_conv_cpb_w0, L1_conv_cpb_b0, L1_conv_cpb_w1, L1_conv_cpb_b1, L1_conv_cpb_w2, L1_conv_cpb_b2):
    import jax
    import jax.numpy as jnp

    def _L0_conv_ref(x, w_qs, b_qs, w_vs, b_vs, mix_w, w_out, bn_gamma, bn_beta):
        import jax, jax.numpy as jnp
        import numpy as np
        N_HEAD, N_MIX, D_MODEL, D_K, D_V = (8, 2, 128, 16, 16)
        BN_EPS = 1e-05

        def avg_pool_3x3_s2(x):
            win = (1, 1, 3, 3)
            stride = (1, 1, 2, 2)
            pad = [(0, 0), (0, 0), (1, 1), (1, 1)]
            s = jax.lax.reduce_window(x, 0.0, jax.lax.add, win, stride, pad)
            ones = jnp.ones((1, 1, x.shape[2], x.shape[3]), x.dtype)
            cnt = jax.lax.reduce_window(ones, 0.0, jax.lax.add, win, stride, pad)
            return s / cnt

        def conv1x1(x, w, b=None):
            y = jnp.einsum('oc,bchw->bohw', w, x)
            if b is not None:
                y = y + b[None, :, None, None]
            return y
        B, C, H, W = x.shape
        N = H * W
        m = N_MIX
        d = D_K // m
        temperature = D_K ** 0.5
        px = avg_pool_3x3_s2(x)
        N2 = px.shape[2] * px.shape[3]
        qt = conv1x1(x, w_qs, b_qs).reshape(B * N_HEAD, D_K, N)
        kt = conv1x1(px, w_qs, b_qs).reshape(B * N_HEAD, D_K, N2)
        vt = conv1x1(px, w_vs, b_vs).reshape(B * N_HEAD, D_V, N2)
        bar_qt = qt.mean(axis=2)
        pi = jax.nn.softmax(jnp.einsum('md,bd->bm', mix_w, bar_qt), axis=1)
        q = qt.reshape(B * N_HEAD * m, d, N).transpose(0, 2, 1)
        k2 = kt.reshape(B * N_HEAD * m, d, N2)
        attn = jnp.einsum('bnd,bdk->bnk', q, k2) / temperature
        attn = jax.nn.softmax(attn, axis=2)
        attn = (attn * pi.reshape(-1, 1, 1)).reshape(B * N_HEAD, m, N, N2).sum(1)
        out = jnp.einsum('bnk,bvk->bnv', attn, vt)
        out = out.transpose(0, 2, 1).reshape(B, N_HEAD * D_V, H, W)
        out = conv1x1(out, w_out)
        inv = 1.0 / jnp.sqrt(jnp.float32(1.0 + BN_EPS))
        out = out * inv * bn_gamma[None, :, None, None] + bn_beta[None, :, None, None]
        return out + x

    def _L1_conv_ref(x, gamma, w_qkv, w_out, cpb_w0, cpb_b0, cpb_w1, cpb_b1, cpb_w2, cpb_b2):
        import jax, jax.numpy as jnp
        import numpy as np
        ALPHA = 32.0 ** 2
        HEADS = 8
        DIM_HEAD = 16
        EPS = 1e-05

        def _leaky(x):
            return jnp.where(x >= 0, x, 0.1 * x)

        def _cpb_bias(fmap_size, w0, b0, w1, b1, w2, b2):
            pos = jnp.arange(fmap_size)
            gi, gj = jnp.meshgrid(pos, pos, indexing='ij')
            grid = jnp.stack([gi, gj], axis=-1).reshape(-1, 2)
            rel = grid[:, None, :] - grid[None, :, :]
            rel = jnp.sign(rel) * jnp.log(jnp.abs(rel) + 1.0)
            h = _leaky(jnp.einsum('ijc,dc->ijd', rel.astype(jnp.float32), w0) + b0)
            h = _leaky(jnp.einsum('ijc,dc->ijd', h, w1) + b1)
            h = jnp.einsum('ijc,hc->ijh', h, w2) + b2
            return jnp.transpose(h, (2, 0, 1))

        def _stable_softmax(t, alpha=ALPHA):
            t = t / alpha
            t = t - jax.lax.stop_gradient(jnp.max(t, axis=-1, keepdims=True))
            return jax.nn.softmax(t * alpha, axis=-1)
        B, C, H, W = x.shape
        n = H * W
        scale = DIM_HEAD ** (-0.5)
        residual = x
        mean = jnp.mean(x, axis=1, keepdims=True)
        var = jnp.var(x, axis=1, keepdims=True)
        xn = (x - mean) / jnp.sqrt(var + EPS) * gamma
        xf = xn.reshape(B, C, n)
        qkv = jnp.einsum('oc,bcn->bon', w_qkv, xf)
        q, k, v = jnp.split(qkv, 3, axis=1)
        rs = lambda t: t.reshape(B, HEADS, DIM_HEAD, n)
        q, k, v = (rs(q), rs(k), rs(v))
        sim = jnp.einsum('bhdi,bhdj->bhij', q, k) * scale
        bias = _cpb_bias(H, cpb_w0, cpb_b0, cpb_w1, cpb_b1, cpb_w2, cpb_b2)
        sim = sim + bias[None]
        attn = _stable_softmax(sim)
        out = jnp.einsum('bhij,bhdj->bhdi', attn, v)
        out = out.reshape(B, HEADS * DIM_HEAD, n)
        out = jnp.einsum('oc,bcn->bon', w_out, out).reshape(B, C, H, W)
        return out + residual

    def _gn(v, G=32, eps=1e-05):
        B_, C_, H_, W_ = v.shape
        g = v.reshape(B_, G, C_ // G, H_, W_)
        m = jnp.mean(g, axis=(2, 3, 4), keepdims=True)
        s = jnp.var(g, axis=(2, 3, 4), keepdims=True)
        return ((g - m) / jnp.sqrt(s + eps)).reshape(v.shape)

    def _ln_c(v, eps=1e-06):
        m = jnp.mean(v, axis=1, keepdims=True)
        s = jnp.var(v, axis=1, keepdims=True)
        return (v - m) / jnp.sqrt(s + eps)

    def _ln_t(v, eps=1e-05):
        m = jnp.mean(v, axis=-1, keepdims=True)
        s = jnp.var(v, axis=-1, keepdims=True)
        return (v - m) / jnp.sqrt(s + eps)

    def _to_tokens(v):
        B_, C_, H_, W_ = v.shape
        return v.reshape(B_, C_, H_ * W_).transpose(0, 2, 1)

    def _from_tokens(t, like):
        B_, C_, H_, W_ = like.shape
        return t.transpose(0, 2, 1).reshape(B_, C_, H_, W_)
    x = _L0_conv_ref(x, L0_conv_w_qs, L0_conv_b_qs, L0_conv_w_vs, L0_conv_b_vs, L0_conv_mix_w, L0_conv_w_out, L0_conv_bn_gamma, L0_conv_bn_beta)
    x = _L1_conv_ref(x, L1_conv_gamma, L1_conv_w_qkv, L1_conv_w_out, L1_conv_cpb_w0, L1_conv_cpb_b0, L1_conv_cpb_w1, L1_conv_cpb_b1, L1_conv_cpb_w2, L1_conv_cpb_b2)
    return x

_drawn_inputs = setup_inputs


def setup_inputs(seed=0):
    import zlib

    import numpy as np

    out = dict(_drawn_inputs(seed))
    spreads = {'L0_conv_b_qs': (0.0, 0.8),
     'L0_conv_b_vs': (0.0, 0.322),
     'L0_conv_bn_gamma': (1.0, 0.6),
     'L0_conv_bn_beta': (0.0, 0.1),
     'L1_conv_gamma': (1.0, 0.6)}
    factors = {'L0_conv_w_qs': 8.0,
     'L0_conv_w_vs': 7.593,
     'L0_conv_mix_w': 8.0,
     'L1_conv_cpb_w0': 28.485,
     'L1_conv_cpb_b0': 56.034,
     'L1_conv_cpb_w1': 23.71,
     'L1_conv_cpb_b1': 64.0,
     'L1_conv_cpb_w2': 27.25,
     'L1_conv_cpb_b2': 64.0}
    for name, (base, spread) in spreads.items():
        noise = np.random.default_rng([zlib.crc32(name.encode()), seed]).standard_normal(out[name].shape)
        drawn = base * np.exp(spread * noise) if base else spread * noise
        out[name] = jnp.asarray(drawn.astype(out[name].dtype))
    for name, factor in factors.items():
        out[name] = (out[name] * factor).astype(out[name].dtype)
    return out
```

```python
import numpy as np
import concourse.bass as bass
from concourse import mybir
from contextlib import ExitStack

F32, F16, BF16 = mybir.dt.float32, mybir.dt.float16, mybir.dt.bfloat16
ALU, ACT, AX = mybir.AluOpType, mybir.ActivationFunctionType, mybir.AxisListType

NB, C, H, W = 2, 128, 56, 56
N = H * W
HP = H // 2
NP = HP * HP
QB = 8 * W
UNITS = H // 8
QT = 2 * W
TILES = QB // QT
HD = 16
MAXROW = 48
D = 2 * H - 1
DR = D + 1
TROWS = 4
TC = TROWS * D
ROUNDS = DR // (4 * TROWS)
BROWS = H + 7
MROWS = H + 6
RING = 2
SLOTS = 4
INV_BN = float(np.float32(1.0) / np.sqrt(np.float32(1.0 + 1e-5)))
LN_EPS = 1e-5

QW, KW, VW, OW, BV, BQ, BK, WG = 0, 256, 512, 576, 704, 768, 770, 772
C_ID, C_SEL, C_FLIP, C_ONE, C_QM, C_KM, C_MEAN, C_EPS, CW = 0, 128, 132, 188, 189, 191, 193, 321, 322
S_W0, S_W1, S_W2, S_B0, S_B1, S_B2, S_WQ, S_BQ, S_GBN, S_BETA, S_GLN, SW = (
    0, 64, 96, 128, 129, 130, 131, 259, 260, 261, 262, 263)
B_SUM, B_MEAN, B_LOG, B_TOP, B_EXP, B_DEN, B_GBN, BW = 0, 2, 4, 20, 28, 44, 52, 53


class Layer:
    def __init__(self, number, groups, key_tiles, key_rows, chunks, chunk):
        self.number, self.groups, self.key_tiles, self.key_rows = number, groups, key_tiles, key_rows
        self.chunks, self.chunk, self.biased = chunks, chunk, number == 1
        self.banks_of_values = key_tiles // 7
        self.work = [(p, t, c) for p in range(2) for t in range(TILES) for c in range(chunks)]
        self.upto = [len(self.work) * k // (key_tiles - 1) for k in range(key_tiles)]


L0 = Layer(0, 4, 7, QT, 2, NP // 2)
L1 = Layer(1, 2, 28, 128, 7, QB)


def settle(eng, sem, count):
    eng.wait_ge(sem, count)
    eng.nop(nofuse=True).then_inc(sem, -count)


def build(nc, x, small, mixes, consts, wg0, wg1, out):
    ctx = ExitStack()
    with ctx:
        def sb(name, shape, dt=F32):
            return ctx.enter_context(nc.sbuf_tensor(name, shape, dt))

        def sem(name):
            return ctx.enter_context(nc.semaphore(name))

        xsrc = sb("xsrc", [C, N])
        xacc = sb("xacc", [C, NB * N])
        cst = sb("cst", [128, CW])
        sml = sb("sml", [128, SW])
        bar = sb("bar", [128, BW])
        pi = sb("pi", [128, 8])
        wg = sb("wg", [128, WG])
        wout = sb("wout", [128, C])
        kbias = sb("kbias", [128, 2])
        keys = sb("keys", [128, 2, 28 * 128], F16)
        vals = sb("vals", [128, 28, 4, HD + 1])
        qs = sb("qs", [128, 2, 2, QB], F16)
        full = sb("full", [128, SLOTS, QB])
        high = sb("high", [128, SLOTS, QB], F16)
        probs = sb("probs", [128, RING, 4, QB])
        junk = sb("junk", [QT, 4, QB], BF16)
        maxes = sb("maxes", [QT, 2, TILES, 2, 7])
        negmax = sb("negmax", [QT, 2, TILES, 128])
        sums = sb("sums", [128, QB])
        scaled = sb("scaled", [128, QB])
        rden = sb("rden", [QT, TILES, 4])
        rwide = sb("rwide", [QT, TILES, 4, 32])
        flip = sb("flip", [QT, W], F16)
        bstage = sb("bstage", [128, 2, 4, BROWS * W], F16)
        mstage = sb("mstage", [128, 2, 2, MROWS * W], BF16)
        P = ctx.enter_context(nc.psum_tensor("P", [128, 8, 512], F32))

        early = mstage[:, :, :, :].rearrange("p a s n -> p (a s n)").bitcast(F32)
        pooled = early[:, 0:NP]
        mix = early[:, 800:800 + 1024]
        pos = early[:, 1824:1824 + 5 * DR].rearrange("p (a n) -> p a n", n=DR)
        tall = early[:, 2400:2400 + H * HP].rearrange("p (y x) -> p y x", x=HP)
        flat = bstage[:, :, :, :].rearrange("p a s n -> p (a s n)")
        tab_hi, tab_lo = flat[:, 0:ROUNDS * TC], flat[:, ROUNDS * TC:2 * ROUNDS * TC]
        tab_bf = flat[:, 2 * ROUNDS * TC:3 * ROUNDS * TC].bitcast(BF16)
        lots = probs[:, :, :, :].rearrange("p a s n -> p (a s) n")

        t_hi = nc.dram_tensor("t_hi", (8, DR * D), F16)
        t_lo = nc.dram_tensor("t_lo", (8, DR * D), F16)
        t_bf = nc.dram_tensor("t_bf", (8, DR * D), BF16)
        g_bias = nc.dram_tensor("g_bias", (8, QT, D * W), F16)
        g_max = nc.dram_tensor("g_max", (8, QT, (D - 1) * W), BF16)

        small_loaded, xacc_loaded, pos_made = sem("small_loaded"), sem("xacc_loaded"), sem("pos_made")
        pos_steps, logs_made = sem("pos_steps"), sem("logs_made")
        net_mm, net_act, net_dve = sem("net_mm"), sem("net_act"), sem("net_dve")
        table_made, table_stored, spread = sem("table_made"), sem("table_stored"), sem("spread")
        sums_of_x, pi_mm, pi_act, pi_dve = sem("sums_of_x"), sem("pi_mm"), sem("pi_act"), sem("pi_dve")
        cleared, pool_steps = sem("cleared"), sem("pool_steps")
        xsrc_loaded, source_ready = sem("xsrc_loaded"), sem("source_ready")
        wg_loaded, wg_ready, group_free = sem("wg_loaded"), sem("wg_ready"), sem("group_free")
        kproj, kfull, khigh = sem("kproj"), sem("kfull"), sem("khigh")
        keys_even, keys_odd = sem("keys_even"), sem("keys_odd")
        vproj, vals_made = sem("vproj"), sem("vals_made")
        ln_mean, ln_cent, ln_sq, ln_var, ln_sd, ln_own = (sem(n) for n in
            ("ln_mean", "ln_cent", "ln_sq", "ln_var", "ln_sd", "ln_own"))
        qproj, qfull, qhigh, qs_made = sem("qproj"), sem("qfull"), sem("qhigh"), sem("qs_made")
        scores_made, max_done = sem("scores_made"), sem("max_done")
        neg_made, neg_turned, shifted = sem("neg_made"), sem("neg_turned"), sem("shifted")
        st_made, exp_done, pv_done, sums_made = sem("st_made"), sem("exp_done"), sem("pv_done"), sem("sums_made")
        den_made, rden_own = sem("den_made"), sem("rden_own")
        rden_made, rden_turned = sem("rden_made"), sem("rden_turned")
        scaled_made, yproj, added = sem("scaled_made"), sem("yproj"), sem("added")
        bias_in, bias_free = [sem("bias_in0"), sem("bias_in1")], [sem("bias_free0"), sem("bias_free1")]
        mbias_in, mbias_free = [sem("mbias_in0"), sem("mbias_in1")], [sem("mbias_free0"), sem("mbias_free1")]
        all_added, out_stored = sem("all_added"), sem("out_stored")

        ident = cst[0:QT, C_ID:C_ID + QT]
        sel = cst[:, C_SEL:C_SEL + 4]
        mean = cst[:, C_MEAN:C_MEAN + 128]

        def key_chunks(ly):
            return (N // QB, QB) if ly.biased else (2, NP // 2)

        def key_columns(ly, p, n, rows):
            if ly.biased:
                return keys[rows, p, n * 512:(n + 1) * 512].rearrange("k (a c) -> k a c", c=64)[:, :, 0:W]
            return keys[rows, p, n * (NP // 2):(n + 1) * (NP // 2)]

        block = ctx.enter_context(nc.Block())

        @block.sync
        def _(sp):
            sp.dma_start(sml[:, :], small).then_inc(small_loaded, 16)
            sp.dma_start(cst[:, :], consts).then_inc(small_loaded, 16)
            sp.dma_start(mix, mixes).then_inc(small_loaded, 16)
            for b in range(NB):
                sp.dma_start(xacc[:, b * N:(b + 1) * N], x[b]).then_inc(xacc_loaded, 16)
            sp.wait_ge(table_made, 3 * ROUNDS)
            for t, tab in ((t_hi, tab_hi), (t_lo, tab_lo), (t_bf, tab_bf)):
                for j in range(4):
                    dst = bass.AP(tensor=t, offset=j * TC, ap=[[DR * D, 8], [4 * TC, ROUNDS], [1, TC]])
                    src = tab[32 * j:32 * j + 8, :].rearrange("h (r c) -> h r c", c=TC)
                    sp.dma_start(dst, src).then_inc(table_stored, 16)

            def group_load(packed, g):
                settle(sp, group_free, 1)
                sp.dma_start(wg[:, :], packed[bass.ds(g, 1)].rearrange("g c n -> c (g n)")).then_inc(wg_loaded, 16)

            with nc.sync.Fori(0, NB) as b:
                settle(sp, group_free, 1)
                sp.dma_start(xsrc[:, :], x[bass.ds(b, 1)].rearrange("b c n -> c (b n)")).then_inc(xsrc_loaded, 16)
                sp.nop(nofuse=True).then_inc(group_free, 1)
                with nc.sync.Fori(0, L0.groups) as g:
                    group_load(wg0, g)
            sp.wait_ge(spread, 8 * 4 * 16)

            def stage(g, u, parity):
                for p in range(2):
                    settle(sp, mbias_free[p], 1)
                    src = g_max[bass.ds(4 * g + 2 * p, 2), :, bass.ds(u * (8 * W), MROWS * W)]
                    sp.dma_start(mstage[0:QT, p, :, :], src.rearrange("s p n -> p s n")).then_inc(mbias_in[p], 16)
                settle(sp, bias_free[parity], 1)
                src = g_bias[bass.ds(4 * g, 4), :, bass.ds(u * (8 * W), BROWS * W)]
                sp.dma_start(bstage[0:QT, parity, :, :], src.rearrange("s p n -> p s n")).then_inc(bias_in[parity], 16)

            with nc.sync.Fori(0, NB) as b:
                with nc.sync.Fori(0, L1.groups) as g:
                    group_load(wg1, g)
                    stage(g, 0, 0)
                    with nc.sync.Fori(0, UNITS // 2) as v:
                        stage(g, 2 * v + 1, 1)
                        stage(g, 2 * v + 2, 0)
            sp.wait_ge(all_added, 1)
            for b in range(NB):
                sp.dma_start(out[b], xacc[:, b * N:(b + 1) * N]).then_inc(out_stored, 16)
            sp.wait_ge(out_stored, NB * 16)

        @block.gpsimd
        def _(pool):
            nc.gpsimd.iota(pos[:, 0, :], pattern=[[1, DR]], base=-(H - 1), channel_multiplier=0,
                           allow_small_or_imprecise_dtypes=True).then_inc(pos_made, 1)

            def highs(ready, done, count, width):
                for i in range(count):
                    pool.wait_ge(ready, i + 1)
                    nc.gpsimd.tensor_copy(high[:, i % SLOTS, 0:width], full[:, i % SLOTS, 0:width]).then_inc(done, 1)
                settle(pool, ready, count)

            def layer(ly):
                with nc.gpsimd.Fori(0, NB) as b:
                    with nc.gpsimd.Fori(0, ly.groups) as g:
                        chunks, width = key_chunks(ly)
                        highs(kfull, khigh, 2 * chunks, width)
                        with nc.gpsimd.Fori(0, UNITS) as u:
                            highs(qfull, qhigh, 2, QB)

            layer(L0)
            layer(L1)

        @block.tensor
        def _(pe):
            mm = nc.tensor.matmul

            pe.wait_ge(small_loaded, 48)
            pe.wait_ge(pos_steps, 3)
            for r in range(ROUNDS):
                for j in range(4):
                    dy = TROWS * (4 * r + j)
                    o = P[32 * j:32 * j + 32, 0, 0:TC].rearrange("h (a c) -> h a c", c=D)
                    q = slice(32 * j, 32 * j + 1)
                    mm(o, sml[q, S_W0:S_W0 + 32], pos[q, 4, dy:dy + TROWS].unsqueeze(2).broadcast_to([1, TROWS, D]),
                       start=True, stop=False)
                    last = mm(o, sml[q, S_W0 + 32:S_W0 + 64], pos[q, 4, 0:D].unsqueeze(1).broadcast_to([1, TROWS, D]),
                              start=False, stop=True)
                last.then_inc(net_mm, 1)
                for depth, w in ((1, S_W1), (2, S_W2)):
                    pe.wait_ge(net_dve, 2 * r + depth)
                    for j in range(4):
                        q = slice(32 * j, 32 * j + 32)
                        last = mm(P[q, depth, 0:TC], sml[q, w:w + 32], lots[q, 4 + depth, 0:TC], start=True, stop=True)
                    last.then_inc(net_mm, 1)

            pe.wait_ge(sums_of_x, 1)
            mm(P[:, 3, 0:2], sml[:, S_WQ:S_WQ + 128], bar[:, B_SUM:B_SUM + 2], start=True, stop=True).then_inc(pi_mm, 1)
            pe.wait_ge(pi_act, 1)
            for k in range(8):
                last = mm(P[:, 4, 2 * k:2 * k + 2], mix[:, 128 * k:128 * k + 128], bar[:, B_MEAN:B_MEAN + 2],
                          start=True, stop=True)
            last.then_inc(pi_mm, 1)

            def pass1(ly, parity, done, upto):
                for i in range(done, upto):
                    p, t, c = ly.work[i]
                    for r in range(2):
                        if i:
                            pe.wait_ge(max_done, 2 * i + r - 1)
                        else:
                            pe.wait_ge(qs_made, 2)
                        rows = slice(64 * r, 64 * r + MAXROW)
                        rhs = key_columns(ly, p, c, rows)
                        o = P[0:QT, 4 + r, 0:ly.chunk]
                        if ly.biased:
                            o = o.rearrange("q (a n) -> q a n", n=W)
                        mm(o, qs[rows, parity, p, t * QT:(t + 1) * QT], rhs, start=True, stop=True).then_inc(scores_made, 1)

            def pass2_scores(ly, parity, kt, p):
                kr = ly.key_rows
                if kt:
                    pe.wait_ge(exp_done, 2 * kt - 1 + p)
                for r in range(2):
                    rows = slice(64 * r, 64 * r + MAXROW + 1)
                    last = mm(P[0:kr, 2 * p + r, 0:QB], keys[rows, p, kt * kr:(kt + 1) * kr], qs[rows, parity, p, :],
                              start=True, stop=not ly.biased, skip_group_check=True)
                if ly.biased:
                    for r in range(2):
                        for e in range(2):
                            at = (H - 1 - 2 * kt - e) * W
                            last = mm(P[64 * e:64 * e + W, 2 * p + r, 0:QB], flip[:, :],
                                      bstage[0:QT, parity, 2 * p + r, at:at + QB], start=False, stop=True,
                                      skip_group_check=True)
                last.then_inc(st_made, 1)

            def pass2_values(ly, kt):
                kr = ly.key_rows
                pe.wait_ge(exp_done, 2 * kt + 2)
                for s in range(4):
                    last = mm(P[32 * s:32 * s + HD + 1, 6, 0:QB], vals[0:kr, kt, s, :], probs[0:kr, kt % RING, s, :],
                              start=(kt == 0), stop=(kt == ly.key_tiles - 1), skip_group_check=True)
                last.then_inc(pv_done, 1)

            def section(ly, unit, parity, first, second):
                other = 1 - parity
                if first:
                    for p in range(2):
                        mm(P[:, 4 + p, 0:QB], wg[:, QW + 128 * p:QW + 128 * p + 128], xsrc[:, bass.ds(unit * QB, QB)],
                           start=True, stop=True).then_inc(qproj, 1)
                done = 0
                if second:
                    if ly.biased:
                        settle(pe, bias_in[other], 16)
                    for kt in range(ly.key_tiles):
                        lo, hi = (ly.upto[kt - 1], ly.upto[kt]) if first and kt else (0, 0)
                        pass2_scores(ly, other, kt, 0)
                        pass1(ly, parity, lo, (lo + hi) // 2)
                        pass2_scores(ly, other, kt, 1)
                        pass1(ly, parity, (lo + hi) // 2, hi)
                        done = hi
                        if kt:
                            pass2_values(ly, kt - 1)
                    pass2_values(ly, ly.key_tiles - 1)
                    settle(pe, exp_done, 2 * ly.key_tiles)
                if first:
                    pass1(ly, parity, done, len(ly.work))
                    settle(pe, qs_made, 2)
                    settle(pe, neg_made, 1)
                    settle(pe, max_done, 2 * len(ly.work))
                    for p in range(2):
                        for t in range(TILES):
                            last = mm(P[:, 4 + p, t * QT:(t + 1) * QT], negmax[:, p, t, :], ident, start=True, stop=True)
                            if ly.biased and (p, t) == (0, 0):
                                last.then_inc(mbias_free[1], 1)
                        last.then_inc(neg_turned, 1)
                if second:
                    settle(pe, sums_made, 1)
                    for t in range(TILES):
                        last = mm(P[0:QT, 7, 4 * t:4 * t + 4], sums[:, t * QT:(t + 1) * QT], sel, start=True, stop=True)
                        if ly.biased and t == 0:
                            last.then_inc(bias_free[other], 1)
                    last.then_inc(den_made, 1)
                    settle(pe, rden_made, 1)
                    for t in range(TILES):
                        last = mm(P[:, 7, t * QT:(t + 1) * QT], rwide[:, t, :, :].rearrange("q s c -> q (s c)"),
                                  ident, start=True, stop=True)
                    last.then_inc(rden_turned, 1)
                    settle(pe, scaled_made, 1)
                    mm(P[:, 7, 0:QB], wout[:, :], scaled[:, :], start=True, stop=True).then_inc(yproj, 1)
                if first:
                    settle(pe, shifted, 2)
                if second:
                    settle(pe, added, 1)

            def group(ly, src):
                settle(pe, wg_ready, 1)
                chunks, width = key_chunks(ly)
                for n in range(chunks):
                    if n >= 2:
                        pe.wait_ge(keys_odd, n - 1)
                    for p in range(2):
                        mm(P[:, (2 * n + p) % 4, 0:width], wg[:, KW + 128 * p:KW + 128 * p + 128],
                           src[:, n * width:(n + 1) * width], start=True, stop=True).then_inc(kproj, 1)
                for kt in range(ly.key_tiles):
                    bank, slot = 4 + kt // 7, kt % 7
                    for e in range(2 if ly.biased else 1):
                        rows = W if ly.biased else QT
                        at = kt * QT + e * W
                        last = mm(P[64 * e:64 * e + rows, bank, 64 * slot:64 * slot + 64], src[:, at:at + rows],
                                  wg[:, VW:VW + 64], start=True, stop=True)
                    if slot == 6:
                        last.then_inc(vproj, 1)
                settle(pe, keys_odd, chunks)
                settle(pe, vals_made, ly.banks_of_values)

            def layer_norm(b):
                for n in range(UNITS):
                    mm(P[:, n, 0:QB], mean, xacc[:, bass.ds(b * N + n * QB, QB)], start=True, stop=True).then_inc(ln_mean, 1)
                for n in range(UNITS):
                    pe.wait_ge(ln_sq, n + 1)
                    mm(P[:, n, 0:QB], mean, lots[:, n, :], start=True, stop=True).then_inc(ln_var, 1)
                settle(pe, ln_sq, UNITS)

            def layer(ly):
                with nc.tensor.Fori(0, NB) as b:
                    if ly.biased:
                        layer_norm(b)
                    settle(pe, source_ready, 1)
                    with nc.tensor.Fori(0, ly.groups) as g:
                        group(ly, xsrc if ly.biased else pooled)
                        section(ly, 0, 0, True, False)
                        with nc.tensor.Fori(0, UNITS // 2) as v:
                            section(ly, 2 * v + 1, 1, True, True)
                            section(ly, 2 * v + 2, 0, True, True)
                        section(ly, UNITS, 1, False, True)

            pe.wait_ge(cleared, 1)
            layer(L0)
            pe.wait_ge(cleared, 2)
            layer(L1)

        @block.scalar
        def _(act):
            A = nc.scalar.activation
            act.wait_ge(small_loaded, 48)
            act.wait_ge(pos_steps, 1)
            A(pos[:, 2, :], pos[:, 1, :], ACT.Ln, bias=1.0).then_inc(logs_made, 1)
            for r in range(ROUNDS):
                for depth, b in ((0, S_B0), (1, S_B1), (2, S_B2)):
                    act.wait_ge(net_mm, 3 * r + depth + 1)
                    A(lots[:, depth, 0:TC], P[:, depth, 0:TC], ACT.Identity, bias=sml[:, b:b + 1]).then_inc(net_act, 1)
            act.wait_ge(table_stored, 3 * 4 * 16)
            for h in range(8):
                base = h * DR * D
                for half, t in enumerate((t_hi, t_lo)):
                    src = bass.AP(tensor=t, offset=base, ap=[[1, W], [D, D], [1, W]])
                    dst = bass.AP(tensor=g_bias, offset=(h * QT + half * W) * D * W, ap=[[D * W, W], [W, D], [1, W]])
                    act.dma_start(dst, src).then_inc(spread, 16)
                for a in range(2):
                    src = bass.AP(tensor=t_bf, offset=base + a * D, ap=[[1, W], [D, D - 1], [1, W]])
                    dst = bass.AP(tensor=g_max, offset=(h * QT + a * W) * (D - 1) * W,
                                  ap=[[(D - 1) * W, W], [W, D - 1], [1, W]])
                    act.dma_start(dst, src).then_inc(spread, 16)
            act.wait_ge(pi_mm, 1)
            A(bar[:, B_MEAN:B_MEAN + 2], P[:, 3, 0:2], ACT.Identity, bias=sml[:, S_BQ:S_BQ + 1], scale=1.0 / N)\
                .then_inc(pi_act, 1)
            act.wait_ge(pi_dve, 4)
            A(bar[:, B_EXP:B_EXP + 16], bar[:, B_LOG:B_LOG + 16], ACT.Exp).then_inc(pi_act, 1)

            def section(ly, first, second):
                kr = ly.key_rows
                if first:
                    for p in range(2):
                        act.wait_ge(qproj, p + 1)
                        A(full[:, p, :], P[:, 4 + p, 0:QB], ACT.Identity, bias=wg[:, BQ + p:BQ + p + 1]).then_inc(qfull, 1)
                    settle(act, qproj, 2)
                if second:
                    for kt in range(ly.key_tiles):
                        for p in range(2):
                            act.wait_ge(st_made, 2 * kt + p + 1)
                            if kt >= RING and p == 0:
                                act.wait_ge(pv_done, kt - RING + 1)
                            A(probs[0:kr, kt % RING, 2 * p:2 * p + 2, :], P[0:kr, 2 * p:2 * p + 2, 0:QB],
                              ACT.Exp).then_inc(exp_done, 1)
                    settle(act, st_made, 2 * ly.key_tiles)
                    settle(act, pv_done, ly.key_tiles)
                    A(sums[:, :], P[:, 6, 0:QB], ACT.Copy).then_inc(sums_made, 1)

            def group(ly):
                chunks, width = key_chunks(ly)
                for n in range(chunks):
                    if n >= 2:
                        act.wait_ge(keys_even, n)
                    for p in range(2):
                        i = 2 * n + p
                        act.wait_ge(kproj, i + 1)
                        A(full[:, i % SLOTS, 0:width], P[:, i % 4, 0:width], ACT.Identity, bias=kbias[:, p:p + 1],
                          scale=HD ** -0.5).then_inc(kfull, 1)
                settle(act, kproj, 2 * chunks)
                settle(act, keys_even, chunks)

            def layer_norm():
                for n in range(UNITS):
                    act.wait_ge(ln_cent, n + 1)
                    A(lots[:, n, :], xsrc[:, n * QB:(n + 1) * QB], ACT.Square).then_inc(ln_sq, 1)
                settle(act, ln_cent, UNITS)
                for n in range(UNITS):
                    act.wait_ge(ln_var, n + 1)
                    A(lots[:, n, :], P[:, n, 0:QB], ACT.Sqrt, bias=cst[:, C_EPS:C_EPS + 1]).then_inc(ln_sd, 1)
                settle(act, ln_var, UNITS)

            def layer(ly):
                with nc.scalar.Fori(0, NB) as b:
                    if ly.biased:
                        layer_norm()
                    with nc.scalar.Fori(0, ly.groups) as g:
                        group(ly)
                        section(ly, True, False)
                        with nc.scalar.Fori(0, UNITS // 2) as v:
                            section(ly, True, True)
                            section(ly, True, True)
                        section(ly, False, True)

            layer(L0)
            layer(L1)

        @block.vector
        def _(dve):
            V = nc.vector
            V.memset(P[:, 6, :], 0.0)
            V.memset(negmax[:, :, :, :], 0.0)
            V.memset(vals[:, :, :, :], 1.0).then_inc(cleared, 1)
            dve.wait_ge(small_loaded, 48)
            V.tensor_copy(flip[:, :], cst[0:QT, C_FLIP:C_FLIP + W])
            V.tensor_scalar(bar[:, B_GBN:B_GBN + 1], sml[:, S_GBN:S_GBN + 1], INV_BN, None, ALU.mult)

            dve.wait_ge(pos_made, 1)
            V.scalar_tensor_tensor(out=pos[:, 1, :], in0=pos[:, 0, :], scalar=-1.0, in1=pos[:, 0, :],
                                   op0=ALU.mult, op1=ALU.max).then_inc(pos_steps, 1)
            V.tensor_scalar(pos[:, 3, :], pos[:, 0, :], 1.0, -1.0, ALU.min, ALU.max).then_inc(pos_steps, 1)
            dve.wait_ge(logs_made, 1)
            dve.wait_ge(pos_steps, 2)
            V.tensor_tensor(pos[:, 4, :], pos[:, 2, :], pos[:, 3, :], ALU.mult).then_inc(pos_steps, 1)

            for r in range(ROUNDS):
                for depth in range(2):
                    dve.wait_ge(net_act, 3 * r + depth + 1)
                    V.scalar_tensor_tensor(out=lots[:, 5 + depth, 0:TC], in0=lots[:, depth, 0:TC], scalar=0.1,
                                           in1=lots[:, depth, 0:TC], op0=ALU.mult, op1=ALU.max).then_inc(net_dve, 1)
                cols = slice(r * TC, (r + 1) * TC)
                dve.wait_ge(net_act, 3 * r + 3)
                V.tensor_copy(tab_hi[:, cols], lots[:, 2, 0:TC]).then_inc(table_made, 1)
                V.tensor_copy(tab_bf[:, cols], lots[:, 2, 0:TC]).then_inc(table_made, 1)
                dve.wait_ge(table_made, 3 * r + 1)
                V.tensor_tensor(tab_lo[:, cols], lots[:, 2, 0:TC], tab_hi[:, cols], ALU.subtract).then_inc(table_made, 1)

            dve.wait_ge(xacc_loaded, 32)
            V.tensor_reduce(out=bar[:, B_SUM:B_SUM + 2], in_=xacc[:, :].rearrange("c (b n) -> c b n", n=N),
                            op=ALU.add, axis=AX.X).then_inc(sums_of_x, 1)
            dve.wait_ge(pi_mm, 2)
            own, partner = slice(B_LOG, B_LOG + 8), slice(B_LOG + 8, B_LOG + 16)
            V.tensor_copy(bar[:, B_LOG:B_LOG + 16], P[:, 4, 0:16]).then_inc(pi_dve, 1)
            dve.wait_ge(pi_dve, 1)
            V.tensor_tensor(bar[:, B_TOP:B_TOP + 8], bar[:, own], bar[:, partner], ALU.max).then_inc(pi_dve, 1)
            dve.wait_ge(pi_dve, 2)
            V.tensor_tensor(bar[:, own], bar[:, own], bar[:, B_TOP:B_TOP + 8], ALU.subtract).then_inc(pi_dve, 1)
            V.tensor_tensor(bar[:, partner], bar[:, partner], bar[:, B_TOP:B_TOP + 8], ALU.subtract).then_inc(pi_dve, 1)
            dve.wait_ge(pi_act, 2)
            V.tensor_tensor(bar[:, B_DEN:B_DEN + 8], bar[:, B_EXP:B_EXP + 8], bar[:, B_EXP + 8:B_EXP + 16], ALU.add)\
                .then_inc(pi_dve, 1)
            dve.wait_ge(pi_dve, 5)
            V.reciprocal(bar[:, B_TOP:B_TOP + 8], bar[:, B_DEN:B_DEN + 8]).then_inc(pi_dve, 1)
            dve.wait_ge(pi_dve, 6)
            V.tensor_tensor(pi[:, :], bar[:, B_EXP:B_EXP + 8], bar[:, B_TOP:B_TOP + 8], ALU.mult).then_inc(pi_dve, 1)
            V.tensor_scalar(xacc[:, :], xacc[:, :], sml[:, S_BETA:S_BETA + 1], None, ALU.add).then_inc(pi_dve, 1)
            dve.wait_ge(pi_dve, 8)
            dve.nop(nofuse=True).then_inc(group_free, 1)

            def section(ly, at, parity, first, second):
                if first:
                    for p in range(2):
                        dve.wait_ge(qhigh, p + 1)
                        V.scalar_tensor_tensor(out=qs[:, parity, p, :], in0=high[:, p, :],
                                               scalar=cst[:, C_QM + ly.number:C_QM + ly.number + 1],
                                               in1=full[:, p, :], op0=ALU.mult, op1=ALU.add).then_inc(qs_made, 1)
                    settle(dve, qhigh, 2)
                    for i, (p, t, c) in enumerate(ly.work):
                        if ly.biased and (t, c) == (0, 0):
                            settle(dve, mbias_in[p], 16)
                        for r in range(2):
                            n = 2 * i + r
                            dve.wait_ge(scores_made, n + 1)
                            top = maxes[:, p, t, r, c:c + 1]
                            if ly.biased:
                                end = (2 * t + H - 1 - 8 * c) * W + W - 1
                                bias = mstage[0:QT, p, r, end:end - QB:-1] if end >= QB else mstage[0:QT, p, r, end::-1]
                                V.tensor_tensor_reduce(out=junk[:, n % 4, :], in0=P[0:QT, 4 + r, 0:QB], in1=bias,
                                                       scale=1.0, scalar=-3.0e38, op0=ALU.add, op1=ALU.max,
                                                       accum_out=top).then_inc(max_done, 1)
                            else:
                                V.tensor_reduce(out=top, in_=P[0:QT, 4 + r, 0:ly.chunk], op=ALU.max, axis=AX.X)\
                                    .then_inc(max_done, 1)
                        if (t, c) == (TILES - 1, ly.chunks - 1):
                            dve.wait_ge(max_done, 2 * i + 2)
                            last = V.tensor_reduce(out=negmax[:, p, :, MAXROW::64], in_=maxes[:, p, :, :, 0:ly.chunks],
                                                   op=ALU.max, axis=AX.X, negate=True)
                            if p:
                                last.then_inc(neg_made, 1)
                            elif ly.biased:
                                last.then_inc(mbias_free[0], 1)
                    settle(dve, scores_made, 2 * len(ly.work))
                    for p in range(2):
                        dve.wait_ge(neg_turned, p + 1)
                        V.tensor_tensor(qs[:, parity, p, :], P[:, 4 + p, 0:QB], qs[:, parity, p, :], ALU.add)\
                            .then_inc(shifted, 1)
                    settle(dve, neg_turned, 2)
                if second:
                    settle(dve, den_made, 1)
                    V.reciprocal(rden[:, :, :], P[0:QT, 7, 0:4 * TILES].rearrange("q (t s) -> q t s", s=4))\
                        .then_inc(rden_own, 1)
                    settle(dve, rden_own, 1)
                    V.tensor_copy(rwide[:, :, :, :], rden[:, :, :].unsqueeze(3).broadcast_to([QT, TILES, 4, 32]))\
                        .then_inc(rden_made, 1)
                    settle(dve, rden_turned, 1)
                    V.tensor_tensor(scaled[:, :], P[:, 7, 0:QB], sums[:, :], ALU.mult).then_inc(scaled_made, 1)
                    settle(dve, yproj, 1)
                    acc = xacc[:, bass.ds(at, QB)]
                    if ly.biased:
                        V.tensor_tensor(acc, P[:, 7, 0:QB], acc, ALU.add).then_inc(added, 1)
                    else:
                        V.scalar_tensor_tensor(out=acc, in0=P[:, 7, 0:QB], scalar=bar[:, B_GBN:B_GBN + 1], in1=acc,
                                               op0=ALU.mult, op1=ALU.add).then_inc(added, 1)

            def group(ly, b, g):
                settle(dve, wg_loaded, 16)
                V.scalar_tensor_tensor(out=kbias[:, :], in0=wg[:, BK:BK + 2], scalar=HD ** -0.5,
                                       in1=cst[:, C_ONE:C_ONE + 1].broadcast_to([128, 2]), op0=ALU.mult, op1=ALU.add)
                if ly.biased:
                    V.tensor_copy(wout[:, :], wg[:, OW:OW + 128]).then_inc(wg_ready, 1)
                else:
                    V.tensor_tensor(wout[:, :], wg[:, OW:OW + 128], pi[:, bass.ds(2 * g + b, 1)].broadcast_to([128, 128]),
                                    ALU.mult).then_inc(wg_ready, 1)
                chunks, width = key_chunks(ly)
                for n in range(chunks):
                    for p in range(2):
                        i = 2 * n + p
                        dve.wait_ge(khigh, i + 1)
                        o, h, f = key_columns(ly, p, n, slice(0, 128)), high[:, i % SLOTS, 0:width], full[:, i % SLOTS, 0:width]
                        if ly.biased:
                            h, f = h.rearrange("k (a c) -> k a c", c=W), f.rearrange("k (a c) -> k a c", c=W)
                        V.scalar_tensor_tensor(out=o, in0=h, scalar=cst[:, C_KM + ly.number:C_KM + ly.number + 1], in1=f,
                                               op0=ALU.mult, op1=ALU.add).then_inc(keys_odd if p else keys_even, 1)
                settle(dve, khigh, 2 * chunks)
                for m in range(ly.banks_of_values):
                    dve.wait_ge(vproj, m + 1)
                    for e in range(2 if ly.biased else 1):
                        rows = slice(64 * e, 64 * e + W) if ly.biased else slice(0, QT)
                        size = W if ly.biased else QT
                        last = V.tensor_tensor(
                            vals[rows, 7 * m:7 * m + 7, :, 0:HD],
                            P[rows, 4 + m, 0:448].rearrange("k (a s d) -> k a s d", s=4, d=HD),
                            wg[rows, BV:BV + 64].rearrange("k (s d) -> k s d", d=HD).unsqueeze(1)
                            .broadcast_to([size, 7, 4, HD]), ALU.add)
                    last.then_inc(vals_made, 1)
                settle(dve, vproj, ly.banks_of_values)

            def pool_source():
                settle(dve, xsrc_loaded, 16)
                img = xsrc[:, :].rearrange("c (y x) -> c y x", x=W)
                px = pooled.rearrange("c (y x) -> c y x", x=HP)
                steps = [
                    lambda: V.tensor_tensor(tall, img[:, :, 0::2], img[:, :, 1::2], ALU.add),
                    lambda: V.tensor_tensor(tall[:, :, 1:HP], tall[:, :, 1:HP], img[:, :, 1:W - 2:2], ALU.add),
                    lambda: V.tensor_tensor(px, tall[:, 0::2, :], tall[:, 1::2, :], ALU.add),
                    lambda: V.tensor_tensor(px[:, 1:HP, :], px[:, 1:HP, :], tall[:, 1:H - 2:2, :], ALU.add),
                    lambda: V.tensor_scalar(pooled, pooled, 1.0 / 9.0, None, ALU.mult),
                    lambda: V.tensor_scalar(px[:, 0, :], px[:, 0, :], 1.5, None, ALU.mult),
                    lambda: V.tensor_scalar(px[:, :, 0], px[:, :, 0], 1.5, None, ALU.mult),
                ]
                for k, step in enumerate(steps):
                    step().then_inc(pool_steps, 1)
                    dve.wait_ge(pool_steps, k + 1)
                settle(dve, pool_steps, len(steps))
                dve.nop(nofuse=True).then_inc(source_ready, 1)

            def layer_norm(b):
                for n in range(UNITS):
                    dve.wait_ge(ln_mean, n + 1)
                    V.tensor_tensor(xsrc[:, n * QB:(n + 1) * QB], xacc[:, bass.ds(b * N + n * QB, QB)], P[:, n, 0:QB],
                                    ALU.subtract).then_inc(ln_cent, 1)
                settle(dve, ln_mean, UNITS)
                for n in range(UNITS):
                    dve.wait_ge(ln_sd, n + 1)
                    V.reciprocal(lots[:, n, :], lots[:, n, :]).then_inc(ln_own, 1)
                settle(dve, ln_sd, UNITS)
                for n in range(UNITS):
                    dve.wait_ge(ln_own, n + 1)
                    cols = slice(n * QB, (n + 1) * QB)
                    last = V.scalar_tensor_tensor(out=xsrc[:, cols], in0=xsrc[:, cols], scalar=sml[:, S_GLN:S_GLN + 1],
                                                  in1=lots[:, n, :], op0=ALU.mult, op1=ALU.mult)
                last.then_inc(source_ready, 1)
                settle(dve, ln_own, UNITS)

            def layer(ly):
                with nc.vector.Fori(0, NB) as b:
                    if ly.biased:
                        layer_norm(b)
                    else:
                        pool_source()
                    with nc.vector.Fori(0, ly.groups) as g:
                        group(ly, b, g)
                        section(ly, 0, 0, True, False)
                        with nc.vector.Fori(0, UNITS // 2) as v:
                            section(ly, b * N + v * (2 * QB), 1, True, True)
                            section(ly, b * N + v * (2 * QB) + QB, 0, True, True)
                        section(ly, b * N + (UNITS - 1) * QB, 1, False, True)
                        dve.drain().then_inc(group_free, 1)

            layer(L0)
            V.memset(keys[:, :, :], 0.0)
            V.memset(vals[:, :, :, :], 0.0).then_inc(ln_own, 1)
            settle(dve, ln_own, 1)
            V.memset(vals[0:W, :, :, HD:HD + 1], 1.0)
            V.memset(vals[64:64 + W, :, :, HD:HD + 1], 1.0).then_inc(cleared, 1)
            for s in (*mbias_free, *bias_free):
                dve.nop(nofuse=True).then_inc(s, 1)
            layer(L1)
            dve.drain().then_inc(all_added, 1)


def kernel(**inputs):
    import numpy as _np
    import concourse.bacc as _bacc
    from concourse import mybir as _mybir
    from concourse.bass_utils import run_bass_kernel_spmd as _run

    a = {k: _np.asarray(v) for k, v in inputs.items()}
    f = _np.float32

    def pack(wq, bq, wk, bk, wv, bv, wo, groups, heads_of, width, part_of):
        blocks = 48 // width if width == 16 else 4
        w = _np.zeros((groups, 128, WG), f)
        for g in range(groups):
            for s in range(4):
                h, part, p, r = heads_of(g, s), part_of(s), s // 2, s % 2
                rows = slice(h * 16 + part * width, h * 16 + part * width + width)
                for k in range(blocks):
                    at = 64 * r + width * k
                    w[g, :, QW + 128 * p + at:QW + 128 * p + at + width] = wq[rows].T
                    w[g, :, KW + 128 * p + at:KW + 128 * p + at + width] = wk[rows].T
                    w[g, at:at + width, BQ + p] = bq[rows]
                    w[g, at:at + width, BK + p] = bk[rows]
                head = slice(h * 16, h * 16 + 16)
                w[g, :, VW + 16 * s:VW + 16 * s + 16] = wv[head].T
                w[g, 32 * s:32 * s + 16, OW:OW + 128] = wo[:, head].T
                w[g, :, BV + 16 * s:BV + 16 * s + 16] = bv[head]
        return w

    zero = _np.zeros(128, f)
    wq, bq = a['L0_conv_w_qs'], a['L0_conv_b_qs']
    wg0 = pack(wq, bq, wq, bq, a['L0_conv_w_vs'], a['L0_conv_b_vs'], a['L0_conv_w_out'], 4,
               lambda g, s: 2 * g + s // 2, 8, lambda s: s % 2)
    qkv = a['L1_conv_w_qkv']
    wg1 = pack(qkv[0:128], zero, qkv[128:256], zero, qkv[256:384], zero, a['L1_conv_w_out'], 2,
               lambda g, s: 4 * g + s, 16, lambda s: 0)

    small = _np.zeros((128, SW), f)
    mixes = _np.zeros((128, 8, 128), f)
    for j in range(4):
        q = slice(32 * j, 32 * j + 32)
        small[32 * j, S_W0:S_W0 + 32] = a['L1_conv_cpb_w0'][:, 0]
        small[32 * j, S_W0 + 32:S_W0 + 64] = a['L1_conv_cpb_w0'][:, 1]
        small[q, S_W1:S_W1 + 32] = a['L1_conv_cpb_w1'].T
        small[q, S_W2:S_W2 + 8] = a['L1_conv_cpb_w2'].T
        small[q, S_B0] = a['L1_conv_cpb_b0']
        small[q, S_B1] = a['L1_conv_cpb_b1']
        small[32 * j:32 * j + 8, S_B2] = a['L1_conv_cpb_b2']
    small[:, S_WQ:S_WQ + 128] = wq.T
    small[:, S_BQ] = bq
    small[:, S_GBN] = a['L0_conv_bn_gamma']
    small[:, S_BETA] = a['L0_conv_bn_beta']
    small[:, S_GLN] = a['L1_conv_gamma'].reshape(128)
    for k in range(2):
        for g in range(4):
            for s in range(4):
                h, m = 2 * g + s // 2, (s % 2) ^ k
                mixes[16 * h:16 * h + 16, 4 * k + g, 32 * s:32 * s + 32] = a['L0_conv_mix_w'][m][:, None]

    consts = _np.zeros((128, CW), f)
    consts[:, C_ID:C_ID + 128] = _np.eye(128, dtype=f)
    for s in range(4):
        consts[32 * s + 16, C_SEL + s] = 1.0
    for half in range(2):
        consts[_np.arange(W) + half * W, C_FLIP + W - 1 - _np.arange(W)] = 1.0
    for r in range(2):
        o = 64 * r
        consts[o + MAXROW, C_ONE] = 1.0
        consts[o + 16:o + 32, C_QM] = -1.0
        consts[o + 32:o + 48, C_QM + 1] = -1.0
        consts[o + 8:o + 16, C_KM] = -1.0
        consts[o + 24:o + 32, C_KM] = -1.0
        consts[o + 16:o + 32, C_KM + 1] = -1.0
    consts[:, C_MEAN:C_MEAN + 128] = 1.0 / 128
    consts[:, C_EPS] = LN_EPS

    arrays = {"in_x": a['x'].reshape(NB, C, N), "in_small": small, "in_mixes": mixes.reshape(128, 1024),
              "in_consts": consts, "in_wg0": wg0, "in_wg1": wg1}
    nc = _bacc.Bacc("TRN2", target_bir_lowering=False, num_devices=1)
    args = [nc.dram_tensor(n, v.shape, _mybir.dt.from_np(v.dtype), kind="ExternalInput").ap() for n, v in arrays.items()]
    args.append(nc.dram_tensor("out_0", (NB, C, N), _mybir.dt.float32, kind="ExternalOutput").ap())
    build(nc, *args)
    r = _run(nc, [arrays], core_ids=[0])
    return r.results[0]["out_0"].reshape(NB, C, H, W)
```

```python
import numpy as np
import concourse.bass as bass
from concourse import mybir
from contextlib import ExitStack

F32, F16, BF16 = mybir.dt.float32, mybir.dt.float16, mybir.dt.bfloat16
ALU, ACT, AX = mybir.AluOpType, mybir.ActivationFunctionType, mybir.AxisListType

NB, C, H, W = 2, 128, 56, 56
N = H * W
HP = H // 2
NP = HP * HP
QB = 8 * W
UNITS = H // 8
QT = 2 * W
TILES = QB // QT
HD = 16
MAXROW = 48
D = 2 * H - 1
DR = D + 1
TROWS = 4
TC = TROWS * D
ROUNDS = DR // (4 * TROWS)
BROWS = H + 7
MROWS = H + 6
HALVES = 4
SPLIT = 31
INV_BN = float(np.float32(1.0) / np.sqrt(np.float32(1.0 + 1e-5)))
LN_EPS = 1e-5

QW, KW, VW, OW, BV, BQ, BK, WG = 0, 256, 512, 576, 704, 768, 770, 772
C_ID, C_SEL, C_FLIP, C_ONE, C_QM, C_KM, C_MEAN, C_EPS, CW = 0, 128, 132, 188, 189, 191, 193, 321, 322
S_W0Y, S_W0X, S_W1, S_W2, S_B0, S_B1, S_B2, S_WQ, S_BQ, S_GBN, S_BETA, S_GLN, SW = (
    0, 128, 256, 384, 512, 513, 514, 515, 643, 644, 645, 646, 647)
B_SUM, B_MEAN, B_LOG, B_TOP, B_EXP, B_DEN, B_GBN, BW = 0, 2, 4, 20, 28, 44, 52, 53


class Layer:
    def __init__(self, number, groups, key_tiles, key_rows, chunks, chunk):
        self.number, self.groups, self.key_tiles, self.key_rows = number, groups, key_tiles, key_rows
        self.chunks, self.chunk, self.biased = chunks, chunk, number == 1
        self.banks_of_values = key_tiles // 7
        self.slots = 2 * key_tiles
        self.work = [(p, t, c) for p in range(2) for t in range(TILES) for c in range(chunks)]
        self.upto = [min(len(self.work), -(-len(self.work) * (k + 1) // (self.slots - 2))) for k in range(self.slots)]

    def ring(self, kt):
        return 2 if self.key_tiles % 2 and kt == self.key_tiles - 1 else kt % 2

    def values_before(self, kt, tail):
        for back in range(1, self.key_tiles + 1):
            if self.ring((kt - back) % self.key_tiles) == self.ring(kt):
                break
        before = kt - back
        return before + 1 + tail if before >= 0 else (1 if before == -1 and tail else 0)


L0 = Layer(0, 4, 7, QT, 2, NP // 2)
L1 = Layer(1, 2, 28, 128, 7, QB)


def settle(eng, sem, count):
    eng.wait_ge(sem, count)
    eng.nop(nofuse=True).then_inc(sem, -count)


def build(nc, x, small, mixes, consts, wg0, wg1, out):
    ctx = ExitStack()
    with ctx:
        def sb(name, shape, dt=F32):
            return ctx.enter_context(nc.sbuf_tensor(name, shape, dt))

        def sem(name):
            return ctx.enter_context(nc.semaphore(name))

        xsrc = sb("xsrc", [C, N])
        xacc = sb("xacc", [C, NB * N])
        cst = sb("cst", [128, CW])
        sml = sb("sml", [128, SW])
        bar = sb("bar", [128, BW])
        pi = sb("pi", [128, 8])
        wg = sb("wg", [128, WG])
        wout = sb("wout", [128, C])
        kbias = sb("kbias", [128, 2])
        keys = sb("keys", [128, 2, 28 * 128], F16)
        vals = sb("vals", [128, 28, 4, HD + 1])
        q_next = sb("q_next", [128, 2, QB], F16)
        q_one = sb("q_one", [128, 2, QB], F16)
        q_kept = sb("q_kept", [128, 2, QB], F16)
        q_two = sb("q_two", [128, 2, QB], F16)
        high = sb("high", [128, HALVES, QB], F16)
        eye16 = sb("eye16", [128, 128], F16)
        less_q = sb("less_q", [128, 128], F16)
        less_k = sb("less_k", [128, 128], F16)
        probs = sb("probs", [128, 3, 4, QB])
        junk = sb("junk", [QT, 4, QB], BF16)
        maxes = sb("maxes", [QT, 2, TILES, 2, 7])
        negmax = sb("negmax", [QT, 2, TILES, 128])
        sums = sb("sums", [128, QB])
        scaled = sb("scaled", [128, QB])
        rden = sb("rden", [QT, TILES, 4])
        rwide = sb("rwide", [QT, TILES, 4, 32])
        flip = sb("flip", [QT, W], F16)
        bstage = sb("bstage", [128, 4, BROWS * W], F16)
        mstage = sb("mstage", [128, 2, 2, MROWS * W], BF16)
        P = ctx.enter_context(nc.psum_tensor("P", [128, 8, 512], F32))

        early = mstage[:, :, :, :].rearrange("p a s n -> p (a s n)").bitcast(F32)
        pooled = early[:, 0:NP]
        mix = early[:, 800:800 + 1024]
        pos = early[:, 1824:1824 + 5 * DR].rearrange("p (a n) -> p a n", n=DR)
        posq = early[:, 4000:4000 + 4 * ROUNDS]
        tall = early[:, 2400:2400 + H * HP].rearrange("p (y x) -> p y x", x=HP)
        flat = bstage[:, :, :].rearrange("p s n -> p (s n)")
        tab_hi, tab_lo = flat[:, 0:ROUNDS * TC], flat[:, ROUNDS * TC:2 * ROUNDS * TC]
        tab_bf = flat[:, 2 * ROUNDS * TC:3 * ROUNDS * TC].bitcast(BF16)
        lots = probs[:, :, :, :].rearrange("p a s n -> p (a s) n")

        t_hi = nc.dram_tensor("t_hi", (8, DR * D), F16)
        t_lo = nc.dram_tensor("t_lo", (8, DR * D), F16)
        t_bf = nc.dram_tensor("t_bf", (8, DR * D), BF16)
        g_bias = nc.dram_tensor("g_bias", (8, QT, D * W), F16)
        g_max = nc.dram_tensor("g_max", (8, QT, (D - 1) * W), BF16)

        small_loaded, xacc_loaded, pos_made = sem("small_loaded"), sem("xacc_loaded"), sem("pos_made")
        pos_steps, logs_made = sem("pos_steps"), sem("logs_made")
        net_mm, net_act, net_dve = sem("net_mm"), sem("net_act"), sem("net_dve")
        table_made, table_stored, spread = sem("table_made"), sem("table_stored"), sem("spread")
        sums_of_x, pi_mm, pi_act, pi_dve = sem("sums_of_x"), sem("pi_mm"), sem("pi_act"), sem("pi_dve")
        cleared, pool_steps = sem("cleared"), sem("pool_steps")
        xsrc_loaded, source_ready = sem("xsrc_loaded"), sem("source_ready")
        wg_loaded, wg_ready, group_free = sem("wg_loaded"), sem("wg_ready"), sem("group_free")
        kproj, khigh, kmasked = sem("kproj"), sem("khigh"), sem("kmasked")
        keys_made, vproj, vals_made = sem("keys_made"), sem("vproj"), sem("vals_made")
        ln_mean, ln_cent, ln_sq, ln_var, ln_sd, ln_own = (sem(n) for n in
            ("ln_mean", "ln_cent", "ln_sq", "ln_var", "ln_sd", "ln_own"))
        qproj, qhigh, qmasked = sem("qproj"), sem("qhigh"), sem("qmasked")
        q_first, q_both, q_handed = sem("q_first"), sem("q_both"), sem("q_handed")
        scores_made, max_done, neg_made = sem("scores_made"), sem("max_done"), sem("neg_made")
        kept_own = sem("kept_own")
        neg_turned, shifted = sem("neg_turned"), sem("shifted")
        st_made, exp_done = sem("st_made"), [sem("exp_done0"), sem("exp_done1")]
        pv_done, sums_made = sem("pv_done"), sem("sums_made")
        den_made, rden_own = sem("den_made"), sem("rden_own")
        rden_made, rden_turned = sem("rden_made"), sem("rden_turned")
        scaled_made, yproj, added = sem("scaled_made"), sem("yproj"), sem("added")
        upper_in, upper_free = sem("upper_in"), sem("upper_free")
        lower_in, lower_free = sem("lower_in"), sem("lower_free")
        mbias_in, mbias_free = [sem("mbias_in0"), sem("mbias_in1")], [sem("mbias_free0"), sem("mbias_free1")]
        all_added, out_stored = sem("all_added"), sem("out_stored")

        ident = cst[0:QT, C_ID:C_ID + QT]
        sel = cst[:, C_SEL:C_SEL + 4]
        mean = cst[:, C_MEAN:C_MEAN + 128]

        def key_chunks(ly):
            return (N // QB, QB) if ly.biased else (2, NP // 2)

        def key_columns(ly, p, n, rows):
            if ly.biased:
                return keys[rows, p, n * 512:(n + 1) * 512].rearrange("k (a c) -> k a c", c=64)[:, :, 0:W]
            return keys[rows, p, n * (NP // 2):(n + 1) * (NP // 2)]

        block = ctx.enter_context(nc.Block())

        @block.sync
        def _(sp):
            sp.dma_start(sml[:, :], small).then_inc(small_loaded, 16)
            sp.dma_start(cst[:, :], consts).then_inc(small_loaded, 16)
            sp.dma_start(mix, mixes).then_inc(small_loaded, 16)
            for b in range(NB):
                sp.dma_start(xacc[:, b * N:(b + 1) * N], x[b]).then_inc(xacc_loaded, 16)
            sp.wait_ge(table_made, 3 * ROUNDS)
            for t, tab in ((t_hi, tab_hi), (t_lo, tab_lo), (t_bf, tab_bf)):
                for j in range(4):
                    dst = bass.AP(tensor=t, offset=j * TC, ap=[[DR * D, 8], [4 * TC, ROUNDS], [1, TC]])
                    src = tab[32 * j:32 * j + 8, :].rearrange("h (r c) -> h r c", c=TC)
                    sp.dma_start(dst, src).then_inc(table_stored, 16)
            sp.wait_ge(table_stored, 3 * 4 * 16)
            for h in range(8):
                base = h * DR * D
                for half, t in enumerate((t_hi, t_lo)):
                    src = bass.AP(tensor=t, offset=base, ap=[[1, W], [D, D], [1, W]])
                    dst = bass.AP(tensor=g_bias, offset=(h * QT + half * W) * D * W, ap=[[D * W, W], [W, D], [1, W]])
                    sp.dma_start(dst, src).then_inc(spread, 16)
                for a in range(2):
                    src = bass.AP(tensor=t_bf, offset=base + a * D, ap=[[1, W], [D, D - 1], [1, W]])
                    dst = bass.AP(tensor=g_max, offset=(h * QT + a * W) * (D - 1) * W,
                                  ap=[[(D - 1) * W, W], [W, D - 1], [1, W]])
                    sp.dma_start(dst, src).then_inc(spread, 16)
            sp.wait_ge(spread, 8 * 4 * 16)

            def stage_max(g, u, p):
                settle(sp, mbias_free[p], 1)
                src = g_max[bass.ds(4 * g + 2 * p, 2), :, bass.ds(u * (8 * W), MROWS * W)]
                sp.dma_start(mstage[0:QT, p, :, :], src.rearrange("s p n -> p s n")).then_inc(mbias_in[p], 16)

            def stage_rows(g, u, lo, hi, free, arrived):
                settle(sp, free, 1)
                src = g_bias[bass.ds(4 * g, 4), :, bass.ds(u * (8 * W) + lo * W, (hi - lo) * W)]
                sp.dma_start(bstage[0:QT, :, lo * W:hi * W], src.rearrange("s p n -> p s n")).then_inc(arrived, 16)

            def stage_upper(g, u):
                stage_rows(g, u, SPLIT, BROWS, upper_free, upper_in)

            def stage_lower(g, u):
                stage_rows(g, u, 0, SPLIT, lower_free, lower_in)

            with nc.sync.Fori(0, NB) as b:
                with nc.sync.Fori(0, L1.groups) as g:
                    stage_max(g, 0, 0)
                    stage_max(g, 0, 1)
                    stage_upper(g, 0)
                    stage_lower(g, 0)
                    stage_max(g, 1, 0)
                    stage_max(g, 1, 1)
                    with nc.sync.Fori(0, UNITS - 2) as a:
                        stage_max(g, a + 2, 0)
                        stage_upper(g, a + 1)
                        stage_max(g, a + 2, 1)
                        stage_lower(g, a + 1)
                    stage_upper(g, UNITS - 1)
                    stage_lower(g, UNITS - 1)
            sp.wait_ge(all_added, 1)
            for b in range(NB):
                sp.dma_start(out[b], xacc[:, b * N:(b + 1) * N]).then_inc(out_stored, 16)
            sp.wait_ge(out_stored, NB * 16)

        @block.gpsimd
        def _(pool):
            nc.gpsimd.iota(pos[:, 0, :], pattern=[[1, DR]], base=-(H - 1), channel_multiplier=0,
                           allow_small_or_imprecise_dtypes=True).then_inc(pos_made, 1)

        @block.tensor
        def _(pe):
            mm = nc.tensor.matmul

            pe.wait_ge(small_loaded, 48)
            pe.wait_ge(sums_of_x, 1)
            mm(P[:, 3, 0:2], sml[:, S_WQ:S_WQ + 128], bar[:, B_SUM:B_SUM + 2], start=True, stop=True).then_inc(pi_mm, 1)
            pe.wait_ge(pi_act, 1)
            for k in range(8):
                last = mm(P[:, 4, 2 * k:2 * k + 2], mix[:, 128 * k:128 * k + 128], bar[:, B_MEAN:B_MEAN + 2],
                          start=True, stop=True)
            last.then_inc(pi_mm, 1)

            pe.wait_ge(pos_steps, 4)
            for r in range(ROUNDS):
                o = P[:, 0, 0:TC].rearrange("h (a c) -> h a c", c=D)
                mm(o, sml[:, S_W0Y:S_W0Y + 128], posq[:, 4 * r:4 * r + 4].unsqueeze(2).broadcast_to([128, TROWS, D]),
                   start=True, stop=False)
                mm(o, sml[0:1, S_W0X:S_W0X + 128], pos[0:1, 4, 0:D].unsqueeze(1).broadcast_to([1, TROWS, D]),
                   start=False, stop=True).then_inc(net_mm, 1)
                for depth, w in ((1, S_W1), (2, S_W2)):
                    pe.wait_ge(net_dve, 2 * r + depth)
                    mm(P[:, depth, 0:TC], sml[:, w:w + 128], lots[:, 4 + depth, 0:TC], start=True, stop=True)\
                        .then_inc(net_mm, 1)


            def pass1(ly, lo, hi):
                for i in range(lo, hi):
                    p, t, c = ly.work[i]
                    if not i:
                        settle(pe, q_handed, 1)
                    for r in range(2):
                        if i:
                            pe.wait_ge(max_done, 2 * i + r - 1)
                        rows = slice(64 * r, 64 * r + MAXROW)
                        rhs = key_columns(ly, p, c, rows)
                        o = P[0:QT, 4 + r, 0:ly.chunk]
                        if ly.biased:
                            o = o.rearrange("q (a n) -> q a n", n=W)
                        mm(o, q_one[rows, p, t * QT:(t + 1) * QT], rhs, start=True, stop=True).then_inc(scores_made, 1)

            def pass2_scores(ly, kt, p, tail):
                kr = ly.key_rows
                if kt:
                    pe.wait_ge(exp_done[p], kt)
                elif tail:
                    settle(pe, exp_done[p], ly.key_tiles)
                for r in range(2):
                    rows = slice(64 * r, 64 * r + MAXROW + 1)
                    last = mm(P[0:kr, 2 * p + r, 0:QB], keys[rows, p, kt * kr:(kt + 1) * kr], q_two[rows, p, :],
                              start=True, stop=not ly.biased, skip_group_check=True)
                if ly.biased:
                    for r in range(2):
                        for e in range(2):
                            at = (H - 1 - 2 * kt - e) * W
                            last = mm(P[64 * e:64 * e + W, 2 * p + r, 0:QB], flip[:, :],
                                      bstage[0:QT, 2 * p + r, at:at + QB], start=False, stop=True,
                                      skip_group_check=True)
                last.then_inc(st_made, 1)

            def pass2_values(ly, kt, freed=None):
                kr = ly.key_rows
                for s in range(4):
                    last = mm(P[32 * s:32 * s + HD + 1, 6, 0:QB], vals[0:kr, kt, s, :], probs[0:kr, ly.ring(kt), s, :],
                              start=(kt == 0), stop=(kt == ly.key_tiles - 1), skip_group_check=True)
                    if s == 0 and freed is not None:
                        last.then_inc(freed, 1)
                last.then_inc(pv_done, 1)

            def tail_values(ly):
                pass2_values(ly, ly.key_tiles - 1, lower_free if ly.biased else None)

            def denominators():
                settle(pe, sums_made, 1)
                for t in range(TILES):
                    last = mm(P[0:QT, 7, 4 * t:4 * t + 4], sums[:, t * QT:(t + 1) * QT], sel, start=True, stop=True)
                last.then_inc(den_made, 1)

            def spread_reciprocals():
                settle(pe, rden_made, 1)
                for t in range(TILES):
                    last = mm(P[:, 7, t * QT:(t + 1) * QT], rwide[:, t, :, :].rearrange("q s c -> q (s c)"),
                              ident, start=True, stop=True)
                last.then_inc(rden_turned, 1)

            def project_out():
                settle(pe, scaled_made, 1)
                mm(P[:, 7, 0:QB], wout[:, :], scaled[:, :], start=True, stop=True).then_inc(yproj, 1)

            def project_q(unit, p, bank, after=None):
                if after is not None:
                    settle(pe, after, 1)
                mm(P[:, bank, 0:QB], wg[:, QW + 128 * p:QW + 128 * p + 128], xsrc[:, bass.ds(unit * QB, QB)],
                   start=True, stop=False, skip_group_check=True).then_inc(qproj, 1)

            def mask_q(p, bank):
                settle(pe, qhigh, 1)
                mm(P[:, bank, 0:QB], less_q[:, :], high[:, p, :], start=False, stop=True,
                   skip_group_check=True).then_inc(qmasked, 1)

            def turn_maxima(p, bank):
                settle(pe, neg_made, 1)
                mm(P[:, bank, 0:QB], eye16[:, :], q_kept[:, p, :], start=True, stop=False, skip_group_check=True)
                for t in range(TILES):
                    last = mm(P[:, bank, t * QT:(t + 1) * QT], negmax[:, p, t, :], ident, start=False, stop=True,
                              skip_group_check=True)
                last.then_inc(neg_turned, 1)

            def section(ly, one, two, tail, query):
                extra = {}
                if tail:
                    extra = {2: denominators, 3: spread_reciprocals, 4: project_out}
                if query is not None:
                    extra[5] = lambda: project_q(query, 0, 7, added if tail else None)
                    extra[6] = lambda: mask_q(0, 7)
                    extra[7] = lambda: project_q(query, 1, 7, q_first)
                    extra[8] = lambda: mask_q(1, 7)
                elif tail:
                    extra[5] = lambda: settle(pe, added, 1)
                for slot in range(ly.slots):
                    kt, p = slot // 2, slot % 2
                    if two:
                        if ly.biased and slot == 0:
                            settle(pe, upper_in, 16)
                        if ly.biased and p == 0 and H - 2 - 2 * kt in (SPLIT - 1, SPLIT - 2):
                            settle(pe, lower_in, 16)
                        if slot == 0:
                            settle(pe, shifted, 1)
                        pass2_scores(ly, kt, p, tail)
                        if slot == 0:
                            settle(pe, shifted, 1)
                    if one:
                        pass1(ly, ly.upto[slot - 1] if slot else 0, ly.upto[slot])
                    if slot in extra:
                        extra[slot]()
                    if one and slot >= ly.slots - 2:
                        turn_maxima(p, 4 if p else 7 if two else 6)
                        if p:
                            settle(pe, max_done, 2 * len(ly.work))
                    if two and p:
                        if kt:
                            past = ly.biased and H - 1 - 2 * kt in (SPLIT - 7, SPLIT - 6)
                            pass2_values(ly, kt - 1, upper_free if past else None)
                        elif tail:
                            tail_values(ly)

            def group(ly, src):
                settle(pe, wg_ready, 1)
                chunks, width = key_chunks(ly)
                for i in range(2 * chunks + 2):
                    if i < 2 * chunks:
                        n, p = i // 2, i % 2
                        if i >= 4:
                            pe.wait_ge(keys_made, i - 3)
                        mm(P[:, i % 4, 0:width], wg[:, KW + 128 * p:KW + 128 * p + 128],
                           src[:, n * width:(n + 1) * width], start=True, stop=False, skip_group_check=True)\
                            .then_inc(kproj, 1)
                    if i >= 2:
                        pe.wait_ge(khigh, i - 1)
                        mm(P[:, (i - 2) % 4, 0:width], less_k[:, :], high[:, (i - 2) % HALVES, 0:width],
                           start=False, stop=True, skip_group_check=True).then_inc(kmasked, 1)
                settle(pe, khigh, 2 * chunks)
                for kt in range(ly.key_tiles):
                    bank, slot = 4 + kt // 7, kt % 7
                    for e in range(2 if ly.biased else 1):
                        rows = W if ly.biased else QT
                        at = kt * QT + e * W
                        last = mm(P[64 * e:64 * e + rows, bank, 64 * slot:64 * slot + 64], src[:, at:at + rows],
                                  wg[:, VW:VW + 64], start=True, stop=True)
                    if slot == 6:
                        last.then_inc(vproj, 1)
                settle(pe, keys_made, 2 * chunks)
                for p in range(2):
                    project_q(0, p, 2 + p)
                for p in range(2):
                    mask_q(p, 2 + p)
                settle(pe, vals_made, ly.banks_of_values)
                settle(pe, q_first, 1)

            def layer_norm(b):
                for n in range(UNITS):
                    mm(P[:, n, 0:QB], mean, xacc[:, bass.ds(b * N + n * QB, QB)], start=True, stop=True).then_inc(ln_mean, 1)
                for n in range(UNITS):
                    pe.wait_ge(ln_sq, n + 1)
                    mm(P[:, n, 0:QB], mean, lots[:, n, :], start=True, stop=True).then_inc(ln_var, 1)
                settle(pe, ln_sq, UNITS)

            def layer(ly):
                with nc.tensor.Fori(0, NB) as b:
                    if ly.biased:
                        layer_norm(b)
                    settle(pe, source_ready, 1)
                    with nc.tensor.Fori(0, ly.groups) as g:
                        group(ly, xsrc if ly.biased else pooled)
                        section(ly, True, False, False, 1)
                        section(ly, True, True, False, 2)
                        with nc.tensor.Fori(1, UNITS - 2) as a:
                            section(ly, True, True, True, a + 2)
                        section(ly, True, True, True, None)
                        section(ly, False, True, True, None)
                        for p in range(2):
                            settle(pe, exp_done[p], ly.key_tiles)
                        tail_values(ly)
                        denominators()
                        spread_reciprocals()
                        project_out()
                        settle(pe, added, 1)

            pe.wait_ge(cleared, 1)
            layer(L0)
            pe.wait_ge(cleared, 2)
            layer(L1)

        @block.scalar
        def _(act):
            A = nc.scalar.activation
            act.wait_ge(small_loaded, 48)
            act.wait_ge(pi_mm, 1)
            A(bar[:, B_MEAN:B_MEAN + 2], P[:, 3, 0:2], ACT.Identity, bias=sml[:, S_BQ:S_BQ + 1], scale=1.0 / N)\
                .then_inc(pi_act, 1)
            act.wait_ge(pi_dve, 4)
            A(bar[:, B_EXP:B_EXP + 16], bar[:, B_LOG:B_LOG + 16], ACT.Exp).then_inc(pi_act, 1)
            act.wait_ge(pos_steps, 1)
            A(pos[:, 2, :], pos[:, 1, :], ACT.Ln, bias=1.0).then_inc(logs_made, 1)
            for r in range(ROUNDS):
                for depth, b in ((0, S_B0), (1, S_B1), (2, S_B2)):
                    act.wait_ge(net_mm, 3 * r + depth + 1)
                    A(lots[:, depth, 0:TC], P[:, depth, 0:TC], ACT.Identity, bias=sml[:, b:b + 1]).then_inc(net_act, 1)

            def copy_sums(nth):
                act.wait_ge(pv_done, nth)
                A(sums[:, :], P[:, 6, 0:QB], ACT.Copy).then_inc(sums_made, 1)

            def high_q(p, bank):
                settle(act, qproj, 1)
                A(high[:, p, :], P[:, bank, 0:QB], ACT.Identity, bias=wg[:, BQ + p:BQ + p + 1]).then_inc(qhigh, 1)

            def stack_q(p, bank):
                settle(act, qmasked, 1)
                A(q_next[:, p, :], P[:, bank, 0:QB], ACT.Identity, bias=wg[:, BQ + p:BQ + p + 1])\
                    .then_inc(q_both if p else q_first, 1)

            def shift(p, bank):
                settle(act, neg_turned, 1)
                A(q_two[:, p, :], P[:, bank, 0:QB], ACT.Copy).then_inc(shifted, 1)

            def section(ly, one, two, tail, query):
                kr = ly.key_rows
                for slot in range(ly.slots):
                    kt, p = slot // 2, slot % 2
                    if one and slot >= ly.slots - 2:
                        shift(p, 4 if p else 7 if two else 6)
                    if two:
                        act.wait_ge(st_made, slot + 1)
                        before = ly.values_before(kt, tail)
                        if before and p == 0:
                            act.wait_ge(pv_done, before)
                        A(probs[0:kr, ly.ring(kt), 2 * p:2 * p + 2, :], P[0:kr, 2 * p:2 * p + 2, 0:QB],
                          ACT.Exp).then_inc(exp_done[p], 1)
                    if tail and slot == 1:
                        copy_sums(1)
                    if query:
                        if slot in (5, 7):
                            high_q(slot // 2 - 2, 7)
                        if slot in (6, 8):
                            stack_q(slot // 2 - 3, 7)
                if two:
                    settle(act, st_made, ly.slots)
                    settle(act, pv_done, ly.key_tiles - 1 + tail)

            def group(ly):
                chunks, width = key_chunks(ly)
                for i in range(2 * chunks):
                    p = i % 2
                    act.wait_ge(kproj, i + 1)
                    A(high[:, i % HALVES, 0:width], P[:, i % 4, 0:width], ACT.Identity, bias=kbias[:, p:p + 1],
                      scale=HD ** -0.5).then_inc(khigh, 1)
                settle(act, kproj, 2 * chunks)
                for p in range(2):
                    high_q(p, 2 + p)
                for p in range(2):
                    stack_q(p, 2 + p)

            def layer_norm():
                for n in range(UNITS):
                    act.wait_ge(ln_cent, n + 1)
                    A(lots[:, n, :], xsrc[:, n * QB:(n + 1) * QB], ACT.Square).then_inc(ln_sq, 1)
                settle(act, ln_cent, UNITS)
                for n in range(UNITS):
                    act.wait_ge(ln_var, n + 1)
                    A(lots[:, n, :], P[:, n, 0:QB], ACT.Sqrt, bias=cst[:, C_EPS:C_EPS + 1]).then_inc(ln_sd, 1)
                settle(act, ln_var, UNITS)

            def layer(ly, packed):
                with nc.scalar.Fori(0, NB) as b:
                    if ly.biased:
                        layer_norm()
                    else:
                        settle(act, group_free, 1)
                        act.dma_start(xsrc[:, :], x[bass.ds(b, 1)].rearrange("b c n -> c (b n)")).then_inc(xsrc_loaded, 16)
                        act.nop(nofuse=True).then_inc(group_free, 1)
                    with nc.scalar.Fori(0, ly.groups) as g:
                        settle(act, group_free, 1)
                        act.dma_start(wg[:, :], packed[bass.ds(g, 1)].rearrange("g c n -> c (g n)")).then_inc(wg_loaded, 16)
                        group(ly)
                        section(ly, True, False, False, True)
                        section(ly, True, True, False, True)
                        with nc.scalar.Fori(1, UNITS - 2) as a:
                            section(ly, True, True, True, True)
                        section(ly, True, True, True, False)
                        section(ly, False, True, True, False)
                        copy_sums(1)
                        settle(act, pv_done, 1)

            layer(L0, wg0)
            layer(L1, wg1)

        @block.vector
        def _(dve):
            V = nc.vector
            V.memset(P[:, 6, :], 0.0)
            V.memset(negmax[:, :, :, :], 0.0)
            V.memset(vals[:, :, :, :], 1.0).then_inc(cleared, 1)
            dve.wait_ge(small_loaded, 48)
            V.tensor_copy(flip[:, :], cst[0:QT, C_FLIP:C_FLIP + W])
            V.tensor_copy(eye16[:, :], cst[:, C_ID:C_ID + 128])
            V.tensor_scalar(bar[:, B_GBN:B_GBN + 1], sml[:, S_GBN:S_GBN + 1], INV_BN, None, ALU.mult)

            dve.wait_ge(xacc_loaded, 32)
            V.tensor_reduce(out=bar[:, B_SUM:B_SUM + 2], in_=xacc[:, :].rearrange("c (b n) -> c b n", n=N),
                            op=ALU.add, axis=AX.X).then_inc(sums_of_x, 1)
            dve.wait_ge(pi_mm, 2)
            own, partner = slice(B_LOG, B_LOG + 8), slice(B_LOG + 8, B_LOG + 16)
            V.tensor_copy(bar[:, B_LOG:B_LOG + 16], P[:, 4, 0:16]).then_inc(pi_dve, 1)
            dve.wait_ge(pi_dve, 1)
            V.tensor_tensor(bar[:, B_TOP:B_TOP + 8], bar[:, own], bar[:, partner], ALU.max).then_inc(pi_dve, 1)
            dve.wait_ge(pi_dve, 2)
            V.tensor_tensor(bar[:, own], bar[:, own], bar[:, B_TOP:B_TOP + 8], ALU.subtract).then_inc(pi_dve, 1)
            V.tensor_tensor(bar[:, partner], bar[:, partner], bar[:, B_TOP:B_TOP + 8], ALU.subtract).then_inc(pi_dve, 1)
            dve.wait_ge(pi_act, 2)
            V.tensor_tensor(bar[:, B_DEN:B_DEN + 8], bar[:, B_EXP:B_EXP + 8], bar[:, B_EXP + 8:B_EXP + 16], ALU.add)\
                .then_inc(pi_dve, 1)
            dve.wait_ge(pi_dve, 5)
            V.reciprocal(bar[:, B_TOP:B_TOP + 8], bar[:, B_DEN:B_DEN + 8]).then_inc(pi_dve, 1)
            dve.wait_ge(pi_dve, 6)
            V.tensor_tensor(pi[:, :], bar[:, B_EXP:B_EXP + 8], bar[:, B_TOP:B_TOP + 8], ALU.mult).then_inc(pi_dve, 1)
            V.tensor_scalar(xacc[:, :], xacc[:, :], sml[:, S_BETA:S_BETA + 1], None, ALU.add).then_inc(pi_dve, 1)
            dve.wait_ge(pi_dve, 8)
            dve.nop(nofuse=True).then_inc(group_free, 1)

            dve.wait_ge(pos_made, 1)
            V.scalar_tensor_tensor(out=pos[:, 1, :], in0=pos[:, 0, :], scalar=-1.0, in1=pos[:, 0, :],
                                   op0=ALU.mult, op1=ALU.max).then_inc(pos_steps, 1)
            V.tensor_scalar(pos[:, 3, :], pos[:, 0, :], 1.0, -1.0, ALU.min, ALU.max).then_inc(pos_steps, 1)
            dve.wait_ge(logs_made, 1)
            dve.wait_ge(pos_steps, 2)
            V.tensor_tensor(pos[:, 4, :], pos[:, 2, :], pos[:, 3, :], ALU.mult).then_inc(pos_steps, 1)

            dve.wait_ge(pos_steps, 3)
            for j in range(4):
                q = slice(32 * j, 32 * j + 32)
                last = V.tensor_copy(posq[q, :].rearrange("p (r a) -> p r a", a=TROWS),
                                     pos[q, 4, :].rearrange("p (r b a) -> p r b a", b=4, a=TROWS)[:, :, j, :])
            last.then_inc(pos_steps, 1)

            for r in range(ROUNDS):
                for depth in range(2):
                    dve.wait_ge(net_act, 3 * r + depth + 1)
                    V.scalar_tensor_tensor(out=lots[:, 5 + depth, 0:TC], in0=lots[:, depth, 0:TC], scalar=0.1,
                                           in1=lots[:, depth, 0:TC], op0=ALU.mult, op1=ALU.max).then_inc(net_dve, 1)
                cols = slice(r * TC, (r + 1) * TC)
                dve.wait_ge(net_act, 3 * r + 3)
                V.tensor_copy(tab_hi[:, cols], lots[:, 2, 0:TC]).then_inc(table_made, 1)
                V.tensor_copy(tab_bf[:, cols], lots[:, 2, 0:TC]).then_inc(table_made, 1)
                dve.wait_ge(table_made, 3 * r + 1)
                V.tensor_tensor(tab_lo[:, cols], lots[:, 2, 0:TC], tab_hi[:, cols], ALU.subtract).then_inc(table_made, 1)


            def reciprocals():
                settle(dve, den_made, 1)
                V.reciprocal(rden[:, :, :], P[0:QT, 7, 0:4 * TILES].rearrange("q (t s) -> q t s", s=4)).then_inc(rden_own, 1)
                settle(dve, rden_own, 1)
                V.tensor_copy(rwide[:, :, :, :], rden[:, :, :].unsqueeze(3).broadcast_to([QT, TILES, 4, 32]))\
                    .then_inc(rden_made, 1)

            def normalise():
                settle(dve, rden_turned, 1)
                V.tensor_tensor(scaled[:, :], P[:, 7, 0:QB], sums[:, :], ALU.mult).then_inc(scaled_made, 1)

            def add_up(ly, at):
                settle(dve, yproj, 1)
                acc = xacc[:, bass.ds(at, QB)]
                if ly.biased:
                    V.tensor_tensor(acc, P[:, 7, 0:QB], acc, ALU.add).then_inc(added, 1)
                else:
                    V.scalar_tensor_tensor(out=acc, in0=P[:, 7, 0:QB], scalar=bar[:, B_GBN:B_GBN + 1], in1=acc,
                                           op0=ALU.mult, op1=ALU.add).then_inc(added, 1)

            def hand_queries():
                settle(dve, q_both, 1)
                V.tensor_copy(q_one[:, :, :], q_next[:, :, :]).then_inc(q_handed, 1)

            def pass1(ly, lo, hi, query):
                for i in range(lo, hi):
                    p, t, c = ly.work[i]
                    if ly.biased and (t, c) == (0, 0):
                        settle(dve, mbias_in[p], 16)
                    for r in range(2):
                        n = 2 * i + r
                        dve.wait_ge(scores_made, n + 1)
                        top = maxes[:, p, t, r, c:c + 1]
                        if ly.biased:
                            end = (2 * t + H - 1 - 8 * c) * W + W - 1
                            bias = mstage[0:QT, p, r, end:end - QB:-1] if end >= QB else mstage[0:QT, p, r, end::-1]
                            V.tensor_tensor_reduce(out=junk[:, n % 4, :], in0=P[0:QT, 4 + r, 0:QB], in1=bias,
                                                   scale=1.0, scalar=-3.0e38, op0=ALU.add, op1=ALU.max,
                                                   accum_out=top).then_inc(max_done, 1)
                        else:
                            V.tensor_reduce(out=top, in_=P[0:QT, 4 + r, 0:ly.chunk], op=ALU.max, axis=AX.X)\
                                .then_inc(max_done, 1)
                    if (t, c) == (TILES - 1, ly.chunks - 1):
                        V.tensor_copy(q_kept[:, p, :], q_one[:, p, :]).then_inc(kept_own, 1)
                        settle(dve, kept_own, 1)
                        if ly.biased:
                            dve.nop(nofuse=True).then_inc(mbias_free[p], 1)
                        dve.wait_ge(max_done, 2 * i + 2)
                        V.tensor_reduce(out=negmax[:, p, :, MAXROW::64], in_=maxes[:, p, :, :, 0:ly.chunks],
                                        op=ALU.max, axis=AX.X, negate=True).then_inc(neg_made, 1)
                        if p:
                            settle(dve, scores_made, 2 * len(ly.work))
                            if query:
                                hand_queries()

            def section(ly, at, one, two, tail, query):
                for slot in range(ly.slots):
                    if one:
                        pass1(ly, ly.upto[slot - 1] if slot else 0, ly.upto[slot], query)
                    if tail and slot == 2:
                        reciprocals()
                    if tail and slot == 3:
                        normalise()
                    if tail and slot == 4:
                        add_up(ly, at)

            def group(ly, b, g):
                settle(dve, wg_loaded, 16)
                V.scalar_tensor_tensor(out=kbias[:, :], in0=wg[:, BK:BK + 2], scalar=HD ** -0.5,
                                       in1=cst[:, C_ONE:C_ONE + 1].broadcast_to([128, 2]), op0=ALU.mult, op1=ALU.add)
                if ly.biased:
                    V.tensor_copy(wout[:, :], wg[:, OW:OW + 128]).then_inc(wg_ready, 1)
                else:
                    V.tensor_tensor(wout[:, :], wg[:, OW:OW + 128], pi[:, bass.ds(2 * g + b, 1)].broadcast_to([128, 128]),
                                    ALU.mult).then_inc(wg_ready, 1)
                chunks, width = key_chunks(ly)
                for n in range(chunks):
                    for p in range(2):
                        i = 2 * n + p
                        dve.wait_ge(kmasked, i + 1)
                        o, f = key_columns(ly, p, n, slice(0, 128)), P[:, i % 4, 0:width]
                        if ly.biased:
                            f = f.rearrange("k (a c) -> k a c", c=W)
                        V.tensor_scalar(o, f, HD ** -0.5, kbias[:, p:p + 1], ALU.mult, ALU.add).then_inc(keys_made, 1)
                settle(dve, kmasked, 2 * chunks)
                for m in range(ly.banks_of_values):
                    dve.wait_ge(vproj, m + 1)
                    for e in range(2 if ly.biased else 1):
                        rows = slice(64 * e, 64 * e + W) if ly.biased else slice(0, QT)
                        size = W if ly.biased else QT
                        last = V.tensor_tensor(
                            vals[rows, 7 * m:7 * m + 7, :, 0:HD],
                            P[rows, 4 + m, 0:448].rearrange("k (a s d) -> k a s d", s=4, d=HD),
                            wg[rows, BV:BV + 64].rearrange("k (s d) -> k s d", d=HD).unsqueeze(1)
                            .broadcast_to([size, 7, 4, HD]), ALU.add)
                    last.then_inc(vals_made, 1)
                settle(dve, vproj, ly.banks_of_values)
                hand_queries()

            def masks(ly):
                V.tensor_scalar(less_q[:, :], cst[:, C_ID:C_ID + 128], cst[:, C_QM + ly.number:C_QM + ly.number + 1],
                                None, ALU.mult)
                V.tensor_scalar(less_k[:, :], cst[:, C_ID:C_ID + 128], cst[:, C_KM + ly.number:C_KM + ly.number + 1],
                                HD ** 0.5, ALU.mult, ALU.mult)

            def pool_source():
                settle(dve, xsrc_loaded, 16)
                img = xsrc[:, :].rearrange("c (y x) -> c y x", x=W)
                px = pooled.rearrange("c (y x) -> c y x", x=HP)
                steps = [
                    lambda: V.tensor_tensor(tall, img[:, :, 0::2], img[:, :, 1::2], ALU.add),
                    lambda: V.tensor_tensor(tall[:, :, 1:HP], tall[:, :, 1:HP], img[:, :, 1:W - 2:2], ALU.add),
                    lambda: V.tensor_tensor(px, tall[:, 0::2, :], tall[:, 1::2, :], ALU.add),
                    lambda: V.tensor_tensor(px[:, 1:HP, :], px[:, 1:HP, :], tall[:, 1:H - 2:2, :], ALU.add),
                    lambda: V.tensor_scalar(pooled, pooled, 1.0 / 9.0, None, ALU.mult),
                    lambda: V.tensor_scalar(px[:, 0, :], px[:, 0, :], 1.5, None, ALU.mult),
                    lambda: V.tensor_scalar(px[:, :, 0], px[:, :, 0], 1.5, None, ALU.mult),
                ]
                for k, step in enumerate(steps):
                    step().then_inc(pool_steps, 1)
                    dve.wait_ge(pool_steps, k + 1)
                settle(dve, pool_steps, len(steps))
                dve.nop(nofuse=True).then_inc(source_ready, 1)

            def layer_norm(b):
                for n in range(UNITS):
                    dve.wait_ge(ln_mean, n + 1)
                    V.tensor_tensor(xsrc[:, n * QB:(n + 1) * QB], xacc[:, bass.ds(b * N + n * QB, QB)], P[:, n, 0:QB],
                                    ALU.subtract).then_inc(ln_cent, 1)
                settle(dve, ln_mean, UNITS)
                for n in range(UNITS):
                    dve.wait_ge(ln_sd, n + 1)
                    V.reciprocal(lots[:, n, :], lots[:, n, :]).then_inc(ln_own, 1)
                settle(dve, ln_sd, UNITS)
                for n in range(UNITS):
                    dve.wait_ge(ln_own, n + 1)
                    cols = slice(n * QB, (n + 1) * QB)
                    last = V.scalar_tensor_tensor(out=xsrc[:, cols], in0=xsrc[:, cols], scalar=sml[:, S_GLN:S_GLN + 1],
                                                  in1=lots[:, n, :], op0=ALU.mult, op1=ALU.mult)
                last.then_inc(source_ready, 1)
                settle(dve, ln_own, UNITS)

            def layer(ly):
                with nc.vector.Fori(0, NB) as b:
                    if ly.biased:
                        layer_norm(b)
                    else:
                        pool_source()
                    with nc.vector.Fori(0, ly.groups) as g:
                        group(ly, b, g)
                        section(ly, None, True, False, False, True)
                        section(ly, None, True, True, False, True)
                        with nc.vector.Fori(1, UNITS - 2) as a:
                            section(ly, b * N + (a - 1) * QB, True, True, True, True)
                        section(ly, b * N + (UNITS - 3) * QB, True, True, True, False)
                        section(ly, b * N + (UNITS - 2) * QB, False, True, True, False)
                        reciprocals()
                        normalise()
                        add_up(ly, b * N + (UNITS - 1) * QB)
                        dve.drain().then_inc(group_free, 1)

            masks(L0)
            layer(L0)
            masks(L1)
            V.memset(keys[:, :, :], 0.0)
            V.memset(vals[:, :, :, :], 0.0).then_inc(ln_own, 1)
            settle(dve, ln_own, 1)
            V.memset(vals[0:W, :, :, HD:HD + 1], 1.0)
            V.memset(vals[64:64 + W, :, :, HD:HD + 1], 1.0).then_inc(cleared, 1)
            for s in (*mbias_free, upper_free, lower_free):
                dve.nop(nofuse=True).then_inc(s, 1)
            layer(L1)
            dve.drain().then_inc(all_added, 1)


def kernel(**inputs):
    import numpy as _np
    import concourse.bacc as _bacc
    from concourse import mybir as _mybir
    from concourse.bass_utils import run_bass_kernel_spmd as _run

    a = {k: _np.asarray(v) for k, v in inputs.items()}
    f = _np.float32

    def pack(wq, bq, wk, bk, wv, bv, wo, groups, heads_of, width, part_of):
        blocks = 48 // width if width == 16 else 4
        w = _np.zeros((groups, 128, WG), f)
        for g in range(groups):
            for s in range(4):
                h, part, p, r = heads_of(g, s), part_of(s), s // 2, s % 2
                rows = slice(h * 16 + part * width, h * 16 + part * width + width)
                for k in range(blocks):
                    at = 64 * r + width * k
                    w[g, :, QW + 128 * p + at:QW + 128 * p + at + width] = wq[rows].T
                    w[g, :, KW + 128 * p + at:KW + 128 * p + at + width] = wk[rows].T
                    w[g, at:at + width, BQ + p] = bq[rows]
                    w[g, at:at + width, BK + p] = bk[rows]
                head = slice(h * 16, h * 16 + 16)
                w[g, :, VW + 16 * s:VW + 16 * s + 16] = wv[head].T
                w[g, 32 * s:32 * s + 16, OW:OW + 128] = wo[:, head].T
                w[g, :, BV + 16 * s:BV + 16 * s + 16] = bv[head]
        return w

    zero = _np.zeros(128, f)
    wq, bq = a['L0_conv_w_qs'], a['L0_conv_b_qs']
    wg0 = pack(wq, bq, wq, bq, a['L0_conv_w_vs'], a['L0_conv_b_vs'], a['L0_conv_w_out'], 4,
               lambda g, s: 2 * g + s // 2, 8, lambda s: s % 2)
    qkv = a['L1_conv_w_qkv']
    wg1 = pack(qkv[0:128], zero, qkv[128:256], zero, qkv[256:384], zero, a['L1_conv_w_out'], 2,
               lambda g, s: 4 * g + s, 16, lambda s: 0)

    small = _np.zeros((128, SW), f)
    mixes = _np.zeros((128, 8, 128), f)
    for j in range(4):
        q = slice(32 * j, 32 * j + 32)
        small[32 * j, S_W0Y + 32 * j:S_W0Y + 32 * j + 32] = a['L1_conv_cpb_w0'][:, 0]
        small[0, S_W0X + 32 * j:S_W0X + 32 * j + 32] = a['L1_conv_cpb_w0'][:, 1]
        small[q, S_W1 + 32 * j:S_W1 + 32 * j + 32] = a['L1_conv_cpb_w1'].T
        small[q, S_W2 + 32 * j:S_W2 + 32 * j + 8] = a['L1_conv_cpb_w2'].T
        small[q, S_B0] = a['L1_conv_cpb_b0']
        small[q, S_B1] = a['L1_conv_cpb_b1']
        small[32 * j:32 * j + 8, S_B2] = a['L1_conv_cpb_b2']
    small[:, S_WQ:S_WQ + 128] = wq.T
    small[:, S_BQ] = bq
    small[:, S_GBN] = a['L0_conv_bn_gamma']
    small[:, S_BETA] = a['L0_conv_bn_beta']
    small[:, S_GLN] = a['L1_conv_gamma'].reshape(128)
    for k in range(2):
        for g in range(4):
            for s in range(4):
                h, m = 2 * g + s // 2, (s % 2) ^ k
                mixes[16 * h:16 * h + 16, 4 * k + g, 32 * s:32 * s + 32] = a['L0_conv_mix_w'][m][:, None]

    consts = _np.zeros((128, CW), f)
    consts[:, C_ID:C_ID + 128] = _np.eye(128, dtype=f)
    for s in range(4):
        consts[32 * s + 16, C_SEL + s] = 1.0
    for half in range(2):
        consts[_np.arange(W) + half * W, C_FLIP + W - 1 - _np.arange(W)] = 1.0
    for r in range(2):
        o = 64 * r
        consts[o + MAXROW, C_ONE] = 1.0
        consts[o + 16:o + 32, C_QM] = -1.0
        consts[o + 32:o + 48, C_QM + 1] = -1.0
        consts[o + 8:o + 16, C_KM] = -1.0
        consts[o + 24:o + 32, C_KM] = -1.0
        consts[o + 16:o + 32, C_KM + 1] = -1.0
    consts[:, C_MEAN:C_MEAN + 128] = 1.0 / 128
    consts[:, C_EPS] = LN_EPS

    arrays = {"in_x": a['x'].reshape(NB, C, N), "in_small": small, "in_mixes": mixes.reshape(128, 1024),
              "in_consts": consts, "in_wg0": wg0, "in_wg1": wg1}
    nc = _bacc.Bacc("TRN2", target_bir_lowering=False, num_devices=1)
    args = [nc.dram_tensor(n, v.shape, _mybir.dt.from_np(v.dtype), kind="ExternalInput").ap() for n, v in arrays.items()]
    args.append(nc.dram_tensor("out_0", (NB, C, N), _mybir.dt.float32, kind="ExternalOutput").ap())
    build(nc, *args)
    r = _run(nc, [arrays], core_ids=[0])
    return r.results[0]["out_0"].reshape(NB, C, H, W)
```

```python
import numpy as np
import concourse.bass as bass
from concourse import mybir
from contextlib import ExitStack

F32, F16, BF16 = mybir.dt.float32, mybir.dt.float16, mybir.dt.bfloat16
ALU, ACT, AX = mybir.AluOpType, mybir.ActivationFunctionType, mybir.AxisListType

NB, C, H, W = 2, 128, 56, 56
N = H * W
HP = H // 2
NP = HP * HP
QB = 8 * W
UNITS = H // 8
QT = 2 * W
TILES = QB // QT
HD = 16
MAXROW = 48
D = 2 * H - 1
DR = D + 1
TROWS = 4
TC = TROWS * D
ROUNDS = DR // (4 * TROWS)
BROWS = H + 7
MROWS = H + 6
HALVES = 4
SPLIT = 31
INV_BN = float(np.float32(1.0) / np.sqrt(np.float32(1.0 + 1e-5)))
LN_EPS = 1e-5

QW, KW, VW, OW, BV, BQ, BK, WG = 0, 256, 512, 576, 704, 768, 770, 772
C_ID, C_SEL, C_FLIP, C_ONE, C_QM, C_KM, C_MEAN, C_EPS, CW = 0, 128, 132, 188, 189, 191, 193, 321, 322
S_W0Y, S_W0X, S_W1, S_W2, S_B0, S_B1, S_B2, S_WQ, S_BQ, S_GBN, S_BETA, S_GLN, SW = (
    0, 128, 256, 384, 512, 513, 514, 515, 643, 644, 645, 646, 647)
B_SUM, B_MEAN, B_LOG, B_TOP, B_EXP, B_DEN, B_GBN, BW = 0, 2, 4, 20, 28, 44, 52, 53


NET = [(step - depth, depth) for step in range(ROUNDS + 2) for depth in (2, 1, 0) if 0 <= step - depth < ROUNDS]
NET_HIDDEN = [layer for layer in NET if layer[1] < 2]

FINISH = (2, 3, 4, 5)


class Layer:
    def __init__(self, number, groups, key_tiles, key_rows, chunks, chunk):
        self.number, self.groups, self.key_tiles, self.key_rows = number, groups, key_tiles, key_rows
        self.chunks, self.chunk, self.biased = chunks, chunk, number == 1
        self.banks_of_values = key_tiles // 7
        self.piece = min(key_tiles, 7 - 3 * self.biased)
        self.pieces = key_tiles // self.piece
        self.slots = 2 * key_tiles
        self.work = [(p, t, c) for p in range(2) for t in range(TILES) for c in range(chunks)]
        self.first = self.deal(0, self.slots - 2, (5, 7) if self.biased else (4, 6, 8, 2))

        self.key_parts = 2 * (N // QB) if self.biased else 4
        self.value_slots = {6 + 2 * m: m for m in range(self.banks_of_values)}
        self.first_q = self.key_parts + 1
        self.first_one = self.first_q + 3
        late = range(self.first_one, self.slots - 1)
        self.late = self.deal(self.first_one, self.slots - 1, [k for k in late if k % 2 == self.biased]
                              + [k for k in late if k % 2 != self.biased])

    def deal(self, first, end, more):
        count = [0] * self.slots
        for k in range(first, end):
            count[k] = 1 if self.biased else 2 * (k % 2)
        for n in range(len(self.work) - sum(count)):
            count[more[n % len(more)]] += 1
        done = [sum(count[:k + 1]) for k in range(self.slots)]
        return [(d - (c // 2 if k % 2 else 0), d) for k, (c, d) in enumerate(zip(count, done))]

    def ring(self, kt):
        return 2 if self.key_tiles % 2 and kt == self.key_tiles - 1 else kt % 2

    def values_before(self, kt, tail):
        for back in range(1, self.key_tiles + 1):
            if self.ring((kt - back) % self.key_tiles) == self.ring(kt):
                break
        before = kt - back
        return before + 1 + tail if before >= 0 else (1 if before == -1 and tail else 0)


L0 = Layer(0, 4, 7, QT, 2, NP // 2)
L1 = Layer(1, 2, 28, 128, 7, QB)


def settle(eng, sem, count):
    eng.wait_ge(sem, count)
    eng.nop(nofuse=True).then_inc(sem, -count)


def build(nc, x, small, mixes, consts, wg0, wg1, out):
    ctx = ExitStack()
    with ctx:
        def sb(name, shape, dt=F32):
            return ctx.enter_context(nc.sbuf_tensor(name, shape, dt))

        def sem(name):
            return ctx.enter_context(nc.semaphore(name))

        xsrc = sb("xsrc", [C, N])
        xacc = sb("xacc", [C, NB * N])
        cst = sb("cst", [128, CW])
        sml = sb("sml", [128, SW])
        bar = sb("bar", [128, BW])
        pi = sb("pi", [128, 8])
        wg = sb("wg", [128, WG])
        wout = sb("wout", [128, C])
        kbias = sb("kbias", [128, 2])
        keys_one = sb("keys_one", [128, 2, 28 * 128], F16)
        keys = sb("keys", [128, 2, 28 * 128], F16)
        vals_next = sb("vals_next", [128, 28, 4, HD + 1])
        vals = sb("vals", [128, 28, 4, HD + 1])
        q_next = sb("q_next", [128, 2, QB], F16)
        q_one = sb("q_one", [128, 2, QB], F16)
        q_kept = sb("q_kept", [128, 2, QB], F16)
        q_two = sb("q_two", [128, 2, QB], F16)
        high = sb("high", [128, HALVES, QB], F16)
        eye16 = sb("eye16", [128, 128], F16)
        less_q = sb("less_q", [128, 128], F16)
        less_k = sb("less_k", [128, 128], F16)
        probs = sb("probs", [128, 3, 4, QB])
        junk = sb("junk", [QT, 4, QB], BF16)
        maxes = sb("maxes", [QT, 2, TILES, 2, 7])
        negmax = sb("negmax", [QT, 2, TILES, 128])
        sums = sb("sums", [128, QB])
        scaled = sb("scaled", [128, QB])
        rden = sb("rden", [QT, TILES, 4])
        rwide = sb("rwide", [QT, TILES, 4, 32])
        flip = sb("flip", [QT, W], F16)
        bstage = sb("bstage", [128, 4, BROWS * W], F16)
        mstage = sb("mstage", [128, 2, 2, MROWS * W], BF16)
        P = ctx.enter_context(nc.psum_tensor("P", [128, 8, 512], F32))

        early = mstage[:, :, :, :].rearrange("p a s n -> p (a s n)").bitcast(F32)
        pooled = early[:, 0:NP]
        mix = early[:, 800:800 + 1024]
        pos = early[:, 1824:1824 + 5 * DR].rearrange("p (a n) -> p a n", n=DR)
        posq = early[:, 4000:4000 + 4 * ROUNDS]
        tall = early[:, 2400:2400 + H * HP].rearrange("p (y x) -> p y x", x=HP)
        flat = bstage[:, :, :].rearrange("p s n -> p (s n)")
        tab_hi, tab_lo = flat[:, 0:ROUNDS * TC], flat[:, ROUNDS * TC:2 * ROUNDS * TC]
        tab_bf = flat[:, 2 * ROUNDS * TC:3 * ROUNDS * TC].bitcast(BF16)
        lots = probs[:, :, :, :].rearrange("p a s n -> p (a s) n")

        t_hi = nc.dram_tensor("t_hi", (8, DR * D), F16)
        t_lo = nc.dram_tensor("t_lo", (8, DR * D), F16)
        t_bf = nc.dram_tensor("t_bf", (8, DR * D), BF16)
        g_bias = nc.dram_tensor("g_bias", (8, QT, D * W), F16)
        g_max = nc.dram_tensor("g_max", (8, QT, (D - 1) * W), BF16)

        small_loaded, xacc_loaded, pos_made = sem("small_loaded"), sem("xacc_loaded"), sem("pos_made")
        pos_steps, logs_made = sem("pos_steps"), sem("logs_made")
        net_mm, net_act, net_dve = sem("net_mm"), sem("net_act"), sem("net_dve")
        table_made, table_stored, spread = sem("table_made"), sem("table_stored"), sem("spread")
        sums_of_x, pi_mm, pi_act, pi_dve = sem("sums_of_x"), sem("pi_mm"), sem("pi_act"), sem("pi_dve")
        vals_cleared = sem("vals_cleared")
        cleared, pool_steps = sem("cleared"), sem("pool_steps")
        xsrc_loaded, source_ready = sem("xsrc_loaded"), sem("source_ready")
        wg_loaded, wg_ready, group_free = sem("wg_loaded"), sem("wg_ready"), sem("group_free")
        kproj, khigh, kmasked = sem("kproj"), sem("khigh"), sem("kmasked")
        keys_made, vproj, vals_made = sem("keys_made"), sem("vproj"), sem("vals_made")
        keys_free, vals_free = sem("keys_free"), sem("vals_free")
        keys_handed, vals_handed = sem("keys_handed"), sem("vals_handed")
        output_handed = sem("output_handed")
        ln_mean, ln_cent, ln_sq, ln_var, ln_inv, ln_own = (sem(n) for n in
            ("ln_mean", "ln_cent", "ln_sq", "ln_var", "ln_inv", "ln_own"))
        qproj, qhigh, qmasked = sem("qproj"), sem("qhigh"), sem("qmasked")
        q_first, q_both, q_handed = sem("q_first"), sem("q_both"), sem("q_handed")
        scores_made, max_done, neg_made = sem("scores_made"), sem("max_done"), sem("neg_made")
        kept_own = sem("kept_own")
        neg_turned, shifted = sem("neg_turned"), sem("shifted")
        st_made, exp_done = sem("st_made"), [sem("exp_done0"), sem("exp_done1")]
        pv_done, sums_made = sem("pv_done"), sem("sums_made")
        den_made, rden_own = sem("den_made"), sem("rden_own")
        rden_made, rden_turned = sem("rden_made"), sem("rden_turned")
        scaled_made, yproj, added = sem("scaled_made"), sem("yproj"), sem("added")
        upper_in, upper_free = sem("upper_in"), sem("upper_free")
        lower_in, lower_free = sem("lower_in"), sem("lower_free")
        mbias_in, mbias_free = [sem("mbias_in0"), sem("mbias_in1")], [sem("mbias_free0"), sem("mbias_free1")]
        batch_added, out_stored = sem("batch_added"), sem("out_stored")

        ident = cst[0:QT, C_ID:C_ID + QT]
        sel = cst[:, C_SEL:C_SEL + 4]
        mean = cst[:, C_MEAN:C_MEAN + 128]

        def key_chunks(ly):
            return (N // QB, QB) if ly.biased else (2, NP // 2)

        def key_columns(ly, p, n, rows):
            if ly.biased:
                return keys_one[rows, p, n * 512:(n + 1) * 512].rearrange("k (a c) -> k a c", c=64)[:, :, 0:W]
            return keys_one[rows, p, n * (NP // 2):(n + 1) * (NP // 2)]

        block = ctx.enter_context(nc.Block())

        @block.sync
        def _(sp):
            sp.dma_start(sml[:, :], small).then_inc(small_loaded, 16)
            sp.dma_start(cst[:, :], consts).then_inc(small_loaded, 16)
            sp.dma_start(mix, mixes).then_inc(small_loaded, 16)
            for b in range(NB):
                sp.dma_start(xacc[:, b * N:(b + 1) * N], x[b]).then_inc(xacc_loaded, 16)
            sp.wait_ge(table_made, 3 * ROUNDS)
            for t, tab in ((t_hi, tab_hi), (t_lo, tab_lo), (t_bf, tab_bf)):
                for j in range(4):
                    dst = bass.AP(tensor=t, offset=j * TC, ap=[[DR * D, 8], [4 * TC, ROUNDS], [1, TC]])
                    src = tab[32 * j:32 * j + 8, :].rearrange("h (r c) -> h r c", c=TC)
                    sp.dma_start(dst, src).then_inc(table_stored, 16)
            sp.wait_ge(table_stored, 3 * 4 * 16)
            for h in range(8):
                base = h * DR * D
                for half, t in enumerate((t_hi, t_lo)):
                    src = bass.AP(tensor=t, offset=base, ap=[[1, W], [D, D], [1, W]])
                    dst = bass.AP(tensor=g_bias, offset=(h * QT + half * W) * D * W, ap=[[D * W, W], [W, D], [1, W]])
                    sp.dma_start(dst, src).then_inc(spread, 16)
                for a in range(2):
                    src = bass.AP(tensor=t_bf, offset=base + a * D, ap=[[1, W], [D, D - 1], [1, W]])
                    dst = bass.AP(tensor=g_max, offset=(h * QT + a * W) * (D - 1) * W,
                                  ap=[[(D - 1) * W, W], [W, D - 1], [1, W]])
                    sp.dma_start(dst, src).then_inc(spread, 16)
            sp.wait_ge(spread, 8 * 4 * 16)

            def stage_max(g, u, p):
                settle(sp, mbias_free[p], 1)
                src = g_max[bass.ds(4 * g + 2 * p, 2), :, bass.ds(u * (8 * W), MROWS * W)]
                sp.dma_start(mstage[0:QT, p, :, :], src.rearrange("s p n -> p s n")).then_inc(mbias_in[p], 16)

            def stage_rows(g, u, lo, hi, free, arrived):
                settle(sp, free, 1)
                src = g_bias[bass.ds(4 * g, 4), :, bass.ds(u * (8 * W) + lo * W, (hi - lo) * W)]
                sp.dma_start(bstage[0:QT, :, lo * W:hi * W], src.rearrange("s p n -> p s n")).then_inc(arrived, 16)

            def stage_upper(g, u):
                stage_rows(g, u, SPLIT, BROWS, upper_free, upper_in)

            def stage_lower(g, u):
                stage_rows(g, u, 0, SPLIT, lower_free, lower_in)

            def group_stages(g, after):
                with nc.sync.Fori(0, UNITS - 2) as a:
                    stage_max(g, a + 2, 0)
                    stage_upper(g, a + 1)
                    stage_max(g, a + 2, 1)
                    stage_lower(g, a + 1)
                if after is not None:
                    stage_max(after, 0, 0)
                stage_upper(g, UNITS - 1)
                if after is not None:
                    stage_max(after, 0, 1)
                stage_lower(g, UNITS - 1)
                if after is not None:
                    stage_max(after, 1, 0)
                    stage_upper(after, 0)
                    stage_max(after, 1, 1)
                    stage_lower(after, 0)

            stage_max(0, 0, 0)
            stage_max(0, 0, 1)
            stage_upper(0, 0)
            stage_max(0, 1, 0)
            stage_lower(0, 0)
            stage_max(0, 1, 1)
            for b in range(NB - 1):
                for g in range(L1.groups):
                    group_stages(g, (g + 1) % L1.groups)
                sp.wait_ge(batch_added, b + 1)
                sp.dma_start(out[b], xacc[:, b * N:(b + 1) * N]).then_inc(out_stored, 16)
            for g in range(L1.groups):
                group_stages(g, g + 1 if g + 1 < L1.groups else None)
            sp.wait_ge(batch_added, NB)
            sp.dma_start(out[NB - 1], xacc[:, (NB - 1) * N:NB * N]).then_inc(out_stored, 16)
            sp.wait_ge(out_stored, NB * 16)

        @block.gpsimd
        def _(pool):
            nc.gpsimd.iota(pos[:, 0, :], pattern=[[1, DR]], base=-(H - 1), channel_multiplier=0,
                           allow_small_or_imprecise_dtypes=True).then_inc(pos_made, 1)

        @block.tensor
        def _(pe):
            mm = nc.tensor.matmul

            pe.wait_ge(small_loaded, 48)
            pe.wait_ge(sums_of_x, 1)
            mm(P[:, 3, 0:2], sml[:, S_WQ:S_WQ + 128], bar[:, B_SUM:B_SUM + 2], start=True, stop=True).then_inc(pi_mm, 1)
            pe.wait_ge(pi_act, 1)
            for k in range(8):
                last = mm(P[:, 4, 2 * k:2 * k + 2], mix[:, 128 * k:128 * k + 128], bar[:, B_MEAN:B_MEAN + 2],
                          start=True, stop=True)
            last.then_inc(pi_mm, 1)

            pe.wait_ge(pos_steps, 4)
            for r, depth in NET:
                if r:
                    pe.wait_ge(net_act, NET.index((r - 1, depth)) + 1)
                if depth:
                    pe.wait_ge(net_dve, NET_HIDDEN.index((r, depth - 1)) + 1)
                    w = (S_W1, S_W2)[depth - 1]
                    mm(P[:, depth, 0:TC], sml[:, w:w + 128], lots[:, 4 + depth, 0:TC], start=True, stop=True)\
                        .then_inc(net_mm, 1)
                else:
                    o = P[:, 0, 0:TC].rearrange("h (a c) -> h a c", c=D)
                    rows = posq[:, 4 * r:4 * r + 4].unsqueeze(2).broadcast_to([128, TROWS, D])
                    mm(o, sml[:, S_W0Y:S_W0Y + 128], rows, start=True, stop=False)
                    mm(o, sml[0:1, S_W0X:S_W0X + 128], pos[0:1, 4, 0:D].unsqueeze(1).broadcast_to([1, TROWS, D]),
                       start=False, stop=True).then_inc(net_mm, 1)

            def pass1(ly, lo, hi):
                for i in range(lo, hi):
                    p, t, c = ly.work[i]
                    if not i:
                        settle(pe, q_handed, 1)
                    for r in range(2):
                        if i:
                            pe.wait_ge(max_done, 2 * i + r - 1)
                        rows = slice(64 * r, 64 * r + MAXROW)
                        rhs = key_columns(ly, p, c, rows)
                        o = P[0:QT, 4 + r, 0:ly.chunk]
                        if ly.biased:
                            o = o.rearrange("q (a n) -> q a n", n=W)
                        mm(o, q_one[rows, p, t * QT:(t + 1) * QT], rhs, start=True, stop=True).then_inc(scores_made, 1)

            def pass2_scores(ly, kt, p, tail):
                kr = ly.key_rows
                if kt:
                    pe.wait_ge(exp_done[p], kt)
                elif tail:
                    settle(pe, exp_done[p], ly.key_tiles)
                for r in range(2):
                    rows = slice(64 * r, 64 * r + MAXROW + 1)
                    last = mm(P[0:kr, 2 * p + r, 0:QB], keys[rows, p, kt * kr:(kt + 1) * kr], q_two[rows, p, :],
                              start=True, stop=not ly.biased, skip_group_check=True)
                if not ly.biased:
                    last.then_inc(st_made, 1)

            def pass2_bias(kt, p):
                for r in range(2):
                    for e in range(2):
                        at = (H - 1 - 2 * kt - e) * W
                        last = mm(P[64 * e:64 * e + W, 2 * p + r, 0:QB], flip[:, :],
                                  bstage[0:QT, 2 * p + r, at:at + QB], start=False, stop=True,
                                  skip_group_check=True)
                last.then_inc(st_made, 1)

            def pass2_values(ly, kt, freed=None):
                kr = ly.key_rows
                for s in range(4):
                    last = mm(P[32 * s:32 * s + HD + 1, 6, 0:QB], vals[0:kr, kt, s, :], probs[0:kr, ly.ring(kt), s, :],
                              start=(kt == 0), stop=(kt == ly.key_tiles - 1), skip_group_check=True)
                    if s == 0 and freed is not None:
                        last.then_inc(freed, 1)
                last.then_inc(pv_done, 1)

            def tail_values(ly):
                pass2_values(ly, ly.key_tiles - 1, lower_free if ly.biased else None)

            def denominators():
                settle(pe, sums_made, 1)
                for t in range(TILES):
                    last = mm(P[0:QT, 7, 4 * t:4 * t + 4], sums[:, t * QT:(t + 1) * QT], sel, start=True, stop=True)
                last.then_inc(den_made, 1)

            def spread_reciprocals():
                settle(pe, rden_made, 1)
                for t in range(TILES):
                    last = mm(P[:, 7, t * QT:(t + 1) * QT], rwide[:, t, :, :].rearrange("q s c -> q (s c)"),
                              ident, start=True, stop=True)
                last.then_inc(rden_turned, 1)

            def project_out():
                settle(pe, scaled_made, 1)
                mm(P[:, 7, 0:QB], wout[:, :], scaled[:, :], start=True, stop=True).then_inc(yproj, 1)

            def project_q(unit, p, bank, after=None):
                if after is not None:
                    settle(pe, after, 1)
                mm(P[:, bank, 0:QB], wg[:, QW + 128 * p:QW + 128 * p + 128], xsrc[:, bass.ds(unit * QB, QB)],
                   start=True, stop=False, skip_group_check=True).then_inc(qproj, 1)

            def mask_q(p, bank):
                settle(pe, qhigh, 1)
                mm(P[:, bank, 0:QB], less_q[:, :], high[:, p, :], start=False, stop=True,
                   skip_group_check=True).then_inc(qmasked, 1)

            def turn_maxima(p, bank):
                settle(pe, neg_made, 1)
                mm(P[:, bank, 0:QB], eye16[:, :], q_kept[:, p, :], start=True, stop=False, skip_group_check=True)
                for t in range(TILES):
                    last = mm(P[:, bank, t * QT:(t + 1) * QT], negmax[:, p, t, :], ident, start=False, stop=True,
                              skip_group_check=True)
                last.then_inc(neg_turned, 1)

            def project_keys(ly, src, i, bank):
                chunks, width = key_chunks(ly)
                n, p = i // 2, i % 2
                mm(P[:, bank, 0:width], wg[:, KW + 128 * p:KW + 128 * p + 128], src[:, n * width:(n + 1) * width],
                   start=True, stop=False, skip_group_check=True).then_inc(kproj, 1)

            def mask_keys(ly, i, bank):
                width = key_chunks(ly)[1]
                pe.wait_ge(khigh, i + 1)
                mm(P[:, bank, 0:width], less_k[:, :], high[:, i % HALVES, 0:width], start=False, stop=True,
                   skip_group_check=True).then_inc(kmasked, 1)

            def project_values(ly, src, m, bank):
                for kt in range(7 * m, 7 * m + 7):
                    for e in range(2 if ly.biased else 1):
                        rows = W if ly.biased else QT
                        at, slot = kt * QT + e * W, kt % 7
                        last = mm(P[64 * e:64 * e + rows, bank, 64 * slot:64 * slot + 64], src[:, at:at + rows],
                                  wg[:, VW:VW + 64], start=True, stop=True)
                last.then_inc(vproj, 1)

            def section(ly, one, two, tail, query, src=None, handing=False):
                extra = {}
                dealt = ly.late if src is not None else ly.first
                if tail:
                    extra = dict(zip(FINISH, (denominators, spread_reciprocals, project_out, lambda: settle(pe, added, 1))))
                if query is not None:
                    at = FINISH[3] if src is None else ly.first_one
                    first = [extra[at]] if at in extra else []
                    extra[at] = lambda: [f() for f in first] + [project_q(query, 0, 7)]
                    extra[at + 1] = lambda: mask_q(0, 7)
                    extra[at + 2] = lambda: project_q(query, 1, 7, q_first)
                    extra[at + 3] = lambda: mask_q(1, 7)
                if src is not None:
                    settle(pe, wg_ready, 1)
                for slot in range(ly.slots):
                    kt, p = slot // 2, slot % 2
                    if two:
                        if ly.biased and slot == 0:
                            settle(pe, upper_in, 16)
                        if ly.biased and p == 0 and H - 2 - 2 * kt in (SPLIT - 1, SPLIT - 2):
                            settle(pe, lower_in, 16)
                        if slot == 0:
                            settle(pe, shifted, 1)
                        if handing and p == 0 and kt % ly.piece == 0:
                            pe.wait_ge(keys_handed, kt // ly.piece + 1)
                        pass2_scores(ly, kt, p, tail)
                        between = one and ly.biased and slot and not p
                        if between:
                            pass1(ly, dealt[slot - 1][1], dealt[slot][0])
                        if ly.biased:
                            pass2_bias(kt, p)
                        if slot == 0:
                            settle(pe, shifted, 1)
                    if src is not None:
                        if 1 <= slot <= ly.key_parts:
                            mask_keys(ly, slot - 1, 4 + (slot - 1) % 2)
                        if slot < ly.key_parts:
                            if slot >= 2:
                                pe.wait_ge(keys_made, slot - 1)
                            project_keys(ly, src, slot, 4 + slot % 2)
                        if slot == ly.first_q:
                            settle(pe, khigh, ly.key_parts)
                            settle(pe, keys_made, ly.key_parts)
                            for q in range(2):
                                project_q(0, q, 4 + q)
                        if slot == ly.first_q + 1:
                            for q in range(2):
                                mask_q(q, 4 + q)
                    if src is not None and slot - 2 in ly.value_slots:
                        settle(pe, vals_made, 1)
                    if one and not (two and between):
                        pass1(ly, dealt[slot - 1][1] if slot else 0, dealt[slot][0])
                    if slot in extra:
                        extra[slot]()
                    if src is not None:
                        if slot in ly.value_slots:
                            project_values(ly, src, ly.value_slots[slot], 7)
                        if slot == ly.first_one:
                            settle(pe, q_first, 1)
                    if one and slot >= ly.slots - 2:
                        if two and p == 0 and (src is not None or not ly.biased):
                            pe.wait_ge(exp_done[1], kt)
                        turn_maxima(p, 4 if p else 7 if two else 6)
                        if p:
                            settle(pe, max_done, 2 * len(ly.work))
                    if two and p:
                        if handing and kt and (kt - 1) % ly.piece == 0:
                            pe.wait_ge(vals_handed, (kt - 1) // ly.piece + 1)
                        if kt:
                            past = ly.biased and H - 1 - 2 * kt in (SPLIT - 7, SPLIT - 6)
                            pass2_values(ly, kt - 1, upper_free if past else None)
                        elif tail:
                            tail_values(ly)
                    if one:
                        pass1(ly, *dealt[slot])
                if handing:
                    settle(pe, keys_handed, ly.pieces)
                    settle(pe, vals_handed, ly.pieces)
                    settle(pe, output_handed, 1)

            def prepare(ly, src):
                settle(pe, wg_ready, 1)
                for i in range(ly.key_parts + 2):
                    if i < ly.key_parts:
                        if i >= 4:
                            pe.wait_ge(keys_made, i - 3)
                        project_keys(ly, src, i, i % 4)
                    if i >= 2:
                        mask_keys(ly, i - 2, (i - 2) % 4)
                settle(pe, khigh, ly.key_parts)
                for m in range(ly.banks_of_values):
                    project_values(ly, src, m, 4 + m)
                settle(pe, keys_made, ly.key_parts)
                for p in range(2):
                    project_q(0, p, 2 + p)
                for p in range(2):
                    mask_q(p, 2 + p)
                settle(pe, vals_made, ly.banks_of_values)
                settle(pe, q_first, 1)

            def group(ly, src):
                with nc.tensor.Fori(1, UNITS - 2) as a:
                    section(ly, True, True, True, a + 2)
                section(ly, True, True, True, None)
                section(ly, src is not None, True, True, None if src is None else 1, src)
                if src is not None:
                    section(ly, True, True, True, 2, handing=True)
                    return
                for p in range(2):
                    settle(pe, exp_done[p], ly.key_tiles)
                tail_values(ly)
                denominators()
                spread_reciprocals()
                project_out()
                settle(pe, added, 1)

            def layer_norm(b):
                for n in range(UNITS):
                    mm(P[:, n, 0:QB], mean, xacc[:, bass.ds(b * N + n * QB, QB)], start=True, stop=True).then_inc(ln_mean, 1)
                for n in range(UNITS):
                    pe.wait_ge(ln_sq, n + 1)
                    mm(P[:, n, 0:QB], mean, lots[:, n, :], start=True, stop=True).then_inc(ln_var, 1)
                settle(pe, ln_sq, UNITS)

            def layer(ly):
                with nc.tensor.Fori(0, NB) as b:
                    if ly.biased:
                        layer_norm(b)
                    settle(pe, source_ready, 1)
                    src = xsrc if ly.biased else pooled
                    prepare(ly, src)
                    section(ly, True, False, False, 1)
                    settle(pe, keys_handed, ly.pieces)
                    settle(pe, vals_handed, ly.pieces)
                    settle(pe, output_handed, 1)
                    section(ly, True, True, False, 2)
                    with nc.tensor.Fori(0, ly.groups - 1) as g:
                        group(ly, src)
                    group(ly, None)

            pe.wait_ge(cleared, 1)
            layer(L0)
            pe.wait_ge(cleared, 2)
            layer(L1)

        @block.scalar
        def _(act):
            A = nc.scalar.activation
            act.wait_ge(small_loaded, 48)
            act.wait_ge(pi_mm, 1)
            A(bar[:, B_MEAN:B_MEAN + 2], P[:, 3, 0:2], ACT.Identity, bias=sml[:, S_BQ:S_BQ + 1], scale=1.0 / N)\
                .then_inc(pi_act, 1)
            act.wait_ge(pi_dve, 4)
            A(bar[:, B_EXP:B_EXP + 16], bar[:, B_LOG:B_LOG + 16], ACT.Exp).then_inc(pi_act, 1)
            act.wait_ge(pos_steps, 1)
            A(pos[:, 2, :], pos[:, 1, :], ACT.Ln, bias=1.0).then_inc(logs_made, 1)
            for n, (r, depth) in enumerate(NET):
                act.wait_ge(net_mm, n + 1)
                if r and depth < 2:
                    act.wait_ge(net_dve, NET_HIDDEN.index((r - 1, depth)) + 1)
                elif r:
                    act.wait_ge(table_made, 3 * r)
                b = (S_B0, S_B1, S_B2)[depth]
                A(lots[:, depth, 0:TC], P[:, depth, 0:TC], ACT.Identity, bias=sml[:, b:b + 1]).then_inc(net_act, 1)

            def copy_sums(nth, handing=False):
                act.wait_ge(pv_done, nth)
                if handing:
                    act.nop(nofuse=True).then_inc(vals_free, 1)
                A(sums[:, :], P[:, 6, 0:QB], ACT.Copy).then_inc(sums_made, 1)

            def high_q(p, bank):
                settle(act, qproj, 1)
                A(high[:, p, :], P[:, bank, 0:QB], ACT.Identity, bias=wg[:, BQ + p:BQ + p + 1]).then_inc(qhigh, 1)

            def stack_q(p, bank):
                settle(act, qmasked, 1)
                A(q_next[:, p, :], P[:, bank, 0:QB], ACT.Identity, bias=wg[:, BQ + p:BQ + p + 1])\
                    .then_inc(q_both if p else q_first, 1)

            def shift(p, bank):
                settle(act, neg_turned, 1)
                A(q_two[:, p, :], P[:, bank, 0:QB], ACT.Copy).then_inc(shifted, 1)

            def high_keys(ly, i, bank):
                width, p = key_chunks(ly)[1], i % 2
                act.wait_ge(kproj, i + 1)
                A(high[:, i % HALVES, 0:width], P[:, bank, 0:width], ACT.Identity, bias=kbias[:, p:p + 1],
                  scale=HD ** -0.5).then_inc(khigh, 1)

            def section(ly, one, two, tail, query, following=False, handing=False):
                kr = ly.key_rows

                def queries(slot):
                    at = ly.first_one if following else FINISH[3]
                    if slot in (at, at + 2):
                        high_q((slot - at) // 2, 7)
                    if slot in (at + 1, at + 3):
                        stack_q((slot - at) // 2, 7)

                for slot in range(ly.slots):
                    kt, p = slot // 2, slot % 2
                    if one and slot >= ly.slots - 2:
                        shift(p, 4 if p else 7 if two else 6)
                    if query and following:
                        queries(slot)
                    if two:
                        act.wait_ge(st_made, slot + 1)
                        before = ly.values_before(kt, tail)
                        if before and p == 0:
                            act.wait_ge(pv_done, before)
                        A(probs[0:kr, ly.ring(kt), 2 * p:2 * p + 2, :], P[0:kr, 2 * p:2 * p + 2, 0:QB],
                          ACT.Exp).then_inc(exp_done[p], 1)
                    if tail and slot == 1:
                        copy_sums(1, handing)
                    if query and not following:
                        queries(slot)
                    if following:
                        if slot < ly.key_parts:
                            high_keys(ly, slot, 4 + slot % 2)
                        if slot == ly.first_q - 1:
                            settle(act, kproj, ly.key_parts)
                        if slot == ly.first_q:
                            for q in range(2):
                                high_q(q, 4 + q)
                        if slot == ly.first_q + 1:
                            for q in range(2):
                                stack_q(q, 4 + q)
                if two:
                    settle(act, st_made, ly.slots)
                    if following:
                        act.nop(nofuse=True).then_inc(keys_free, 1)
                    settle(act, pv_done, ly.key_tiles - 1 + tail)

            def prepare(ly):
                for i in range(ly.key_parts):
                    high_keys(ly, i, i % 4)
                settle(act, kproj, ly.key_parts)
                for p in range(2):
                    high_q(p, 2 + p)
                for p in range(2):
                    stack_q(p, 2 + p)

            def load_group(packed, g):
                act.dma_start(wg[:, :], packed[bass.ds(g, 1)].rearrange("g c n -> c (g n)")).then_inc(wg_loaded, 16)

            def group(ly, packed, after):
                with nc.scalar.Fori(1, UNITS - 2) as a:
                    section(ly, True, True, True, True)
                if after is not None:
                    load_group(packed, after)
                section(ly, True, True, True, False)
                section(ly, after is not None, True, True, after is not None, after is not None)
                if after is not None:
                    section(ly, True, True, True, True, handing=True)
                    return
                copy_sums(1)
                settle(act, pv_done, 1)

            def layer_norm():
                for n in range(UNITS):
                    act.wait_ge(ln_cent, n + 1)
                    A(lots[:, n, :], xsrc[:, n * QB:(n + 1) * QB], ACT.Square).then_inc(ln_sq, 1)
                settle(act, ln_cent, UNITS)
                for n in range(UNITS):
                    act.wait_ge(ln_var, n + 1)
                    A(lots[:, n, :], P[:, n, 0:QB], ACT.Ln, bias=cst[:, C_EPS:C_EPS + 1]).then_inc(ln_own, 1)
                settle(act, ln_var, UNITS)
                for n in range(UNITS):
                    act.wait_ge(ln_own, n + 1)
                    A(lots[:, n, :], lots[:, n, :], ACT.Exp, scale=-0.5).then_inc(ln_inv, 1)
                settle(act, ln_own, UNITS)

            def layer(ly, packed):
                with nc.scalar.Fori(0, NB) as b:
                    settle(act, group_free, 1)
                    if not ly.biased:
                        act.dma_start(xsrc[:, :], x[bass.ds(b, 1)].rearrange("b c n -> c (b n)")).then_inc(xsrc_loaded, 16)
                    load_group(packed, 0)
                    if ly.biased:
                        layer_norm()
                    prepare(ly)
                    section(ly, True, False, False, True)
                    section(ly, True, True, False, True)
                    with nc.scalar.Fori(0, ly.groups - 1) as g:
                        group(ly, packed, g + 1)
                    group(ly, packed, None)

            layer(L0, wg0)
            layer(L1, wg1)

        @block.vector
        def _(dve):
            V = nc.vector
            V.memset(P[:, 6, :], 0.0)
            V.memset(negmax[:, :, :, :], 0.0)
            V.memset(vals_next[:, :, :, :], 1.0).then_inc(cleared, 1)
            dve.wait_ge(small_loaded, 48)
            V.tensor_copy(flip[:, :], cst[0:QT, C_FLIP:C_FLIP + W])
            V.tensor_copy(eye16[:, :], cst[:, C_ID:C_ID + 128])
            V.tensor_scalar(bar[:, B_GBN:B_GBN + 1], sml[:, S_GBN:S_GBN + 1], INV_BN, None, ALU.mult)

            dve.wait_ge(xacc_loaded, 32)
            V.tensor_reduce(out=bar[:, B_SUM:B_SUM + 2], in_=xacc[:, :].rearrange("c (b n) -> c b n", n=N),
                            op=ALU.add, axis=AX.X).then_inc(sums_of_x, 1)
            dve.wait_ge(pi_mm, 2)
            own, partner = slice(B_LOG, B_LOG + 8), slice(B_LOG + 8, B_LOG + 16)
            V.tensor_copy(bar[:, B_LOG:B_LOG + 16], P[:, 4, 0:16]).then_inc(pi_dve, 1)
            dve.wait_ge(pi_dve, 1)
            V.tensor_tensor(bar[:, B_TOP:B_TOP + 8], bar[:, own], bar[:, partner], ALU.max).then_inc(pi_dve, 1)
            dve.wait_ge(pi_dve, 2)
            V.tensor_tensor(bar[:, own], bar[:, own], bar[:, B_TOP:B_TOP + 8], ALU.subtract).then_inc(pi_dve, 1)
            V.tensor_tensor(bar[:, partner], bar[:, partner], bar[:, B_TOP:B_TOP + 8], ALU.subtract).then_inc(pi_dve, 1)
            dve.wait_ge(pi_act, 2)
            V.tensor_tensor(bar[:, B_DEN:B_DEN + 8], bar[:, B_EXP:B_EXP + 8], bar[:, B_EXP + 8:B_EXP + 16], ALU.add)\
                .then_inc(pi_dve, 1)
            dve.wait_ge(pi_dve, 5)
            V.reciprocal(bar[:, B_TOP:B_TOP + 8], bar[:, B_DEN:B_DEN + 8]).then_inc(pi_dve, 1)
            dve.wait_ge(pi_dve, 6)
            V.tensor_tensor(pi[:, :], bar[:, B_EXP:B_EXP + 8], bar[:, B_TOP:B_TOP + 8], ALU.mult).then_inc(pi_dve, 1)
            V.tensor_scalar(xacc[:, :], xacc[:, :], sml[:, S_BETA:S_BETA + 1], None, ALU.add).then_inc(pi_dve, 1)
            dve.wait_ge(pi_dve, 8)
            dve.nop(nofuse=True).then_inc(group_free, 1)

            dve.wait_ge(pos_made, 1)
            V.scalar_tensor_tensor(out=pos[:, 1, :], in0=pos[:, 0, :], scalar=-1.0, in1=pos[:, 0, :],
                                   op0=ALU.mult, op1=ALU.max).then_inc(pos_steps, 1)
            V.tensor_scalar(pos[:, 3, :], pos[:, 0, :], 1.0, -1.0, ALU.min, ALU.max).then_inc(pos_steps, 1)
            dve.wait_ge(logs_made, 1)
            dve.wait_ge(pos_steps, 2)
            V.tensor_tensor(pos[:, 4, :], pos[:, 2, :], pos[:, 3, :], ALU.mult).then_inc(pos_steps, 1)

            dve.wait_ge(pos_steps, 3)
            for j in range(4):
                q = slice(32 * j, 32 * j + 32)
                last = V.tensor_copy(posq[q, :].rearrange("p (r a) -> p r a", a=TROWS),
                                     pos[q, 4, :].rearrange("p (r b a) -> p r b a", b=4, a=TROWS)[:, :, j, :])
            last.then_inc(pos_steps, 1)

            for n, (r, depth) in enumerate(NET):
                dve.wait_ge(net_act, n + 1)
                if depth < 2:
                    if r:
                        dve.wait_ge(net_mm, NET.index((r - 1, depth + 1)) + 1)
                    V.scalar_tensor_tensor(out=lots[:, 5 + depth, 0:TC], in0=lots[:, depth, 0:TC], scalar=0.1,
                                           in1=lots[:, depth, 0:TC], op0=ALU.mult, op1=ALU.max).then_inc(net_dve, 1)
                    continue
                cols = slice(r * TC, (r + 1) * TC)
                V.tensor_copy(tab_hi[:, cols], lots[:, 2, 0:TC]).then_inc(table_made, 1)
                V.tensor_copy(tab_bf[:, cols], lots[:, 2, 0:TC]).then_inc(table_made, 1)
                dve.wait_ge(table_made, 3 * r + 1)
                V.tensor_tensor(tab_lo[:, cols], lots[:, 2, 0:TC], tab_hi[:, cols], ALU.subtract).then_inc(table_made, 1)

            def reciprocals():
                settle(dve, den_made, 1)
                V.reciprocal(rden[:, :, :], P[0:QT, 7, 0:4 * TILES].rearrange("q (t s) -> q t s", s=4)).then_inc(rden_own, 1)
                settle(dve, rden_own, 1)
                V.tensor_copy(rwide[:, :, :, :], rden[:, :, :].unsqueeze(3).broadcast_to([QT, TILES, 4, 32]))\
                    .then_inc(rden_made, 1)

            def normalise():
                settle(dve, rden_turned, 1)
                V.tensor_tensor(scaled[:, :], P[:, 7, 0:QB], sums[:, :], ALU.mult).then_inc(scaled_made, 1)

            def add_up(ly, at):
                settle(dve, yproj, 1)
                acc = xacc[:, bass.ds(at, QB)]
                if ly.biased:
                    V.tensor_tensor(acc, P[:, 7, 0:QB], acc, ALU.add).then_inc(added, 1)
                else:
                    V.scalar_tensor_tensor(out=acc, in0=P[:, 7, 0:QB], scalar=bar[:, B_GBN:B_GBN + 1], in1=acc,
                                           op0=ALU.mult, op1=ALU.add).then_inc(added, 1)

            def hand_queries():
                settle(dve, q_both, 1)
                V.tensor_copy(q_one[:, :, :], q_next[:, :, :]).then_inc(q_handed, 1)

            def negate_maxima(ly, p):
                dve.wait_ge(max_done, (p + 1) * len(ly.work))
                if ly.biased:
                    dve.nop(nofuse=True).then_inc(mbias_free[p], 1)
                V.tensor_reduce(out=negmax[:, p, :, MAXROW::64], in_=maxes[:, p, :, :, 0:ly.chunks],
                                op=ALU.max, axis=AX.X, negate=True).then_inc(neg_made, 1)

            def pass1(ly, lo, hi, query):
                for i in range(lo, hi):
                    p, t, c = ly.work[i]
                    if ly.biased and (t, c) == (0, 0):
                        settle(dve, mbias_in[p], 16)
                    for r in range(2):
                        n = 2 * i + r
                        dve.wait_ge(scores_made, n + 1)
                        top = maxes[:, p, t, r, c:c + 1]
                        if ly.biased:
                            end = (2 * t + H - 1 - 8 * c) * W + W - 1
                            bias = mstage[0:QT, p, r, end:end - QB:-1] if end >= QB else mstage[0:QT, p, r, end::-1]
                            V.tensor_tensor_reduce(out=junk[:, n % 4, :], in0=P[0:QT, 4 + r, 0:QB], in1=bias,
                                                   scale=1.0, scalar=-3.0e38, op0=ALU.add, op1=ALU.max,
                                                   accum_out=top).then_inc(max_done, 1)
                        else:
                            V.tensor_reduce(out=top, in_=P[0:QT, 4 + r, 0:ly.chunk], op=ALU.max, axis=AX.X)\
                                .then_inc(max_done, 1)
                    half = len(ly.work) // 2
                    if i == half + 1:
                        V.tensor_copy(q_kept[:, :, :], q_one[:, :, :]).then_inc(kept_own, 1)
                    if i == half + 3:
                        settle(dve, kept_own, 1)
                        negate_maxima(ly, 0)
                    if i == len(ly.work) - 1:
                        negate_maxima(ly, 1)
                        settle(dve, scores_made, 2 * len(ly.work))
                        if query:
                            hand_queries()

            def stack_keys(ly, i, bank):
                width, n, p = key_chunks(ly)[1], i // 2, i % 2
                dve.wait_ge(kmasked, i + 1)
                o, f = key_columns(ly, p, n, slice(0, 128)), P[:, bank, 0:width]
                if ly.biased:
                    f = f.rearrange("k (a c) -> k a c", c=W)
                V.tensor_scalar(o, f, HD ** -0.5, kbias[:, p:p + 1], ALU.mult, ALU.add).then_inc(keys_made, 1)

            def place_values(ly, m, bank):
                settle(dve, vproj, 1)
                for e in range(2 if ly.biased else 1):
                    rows = slice(64 * e, 64 * e + W) if ly.biased else slice(0, QT)
                    size = W if ly.biased else QT
                    last = V.tensor_tensor(
                        vals_next[rows, 7 * m:7 * m + 7, :, 0:HD],
                        P[rows, bank, 0:448].rearrange("k (a s d) -> k a s d", s=4, d=HD),
                        wg[rows, BV:BV + 64].rearrange("k (s d) -> k s d", d=HD).unsqueeze(1)
                        .broadcast_to([size, 7, 4, HD]), ALU.add)
                last.then_inc(vals_made, 1)

            def take_weights():
                settle(dve, wg_loaded, 16)
                V.scalar_tensor_tensor(out=kbias[:, :], in0=wg[:, BK:BK + 2], scalar=HD ** -0.5,
                                       in1=cst[:, C_ONE:C_ONE + 1].broadcast_to([128, 2]), op0=ALU.mult, op1=ALU.add)\
                    .then_inc(wg_ready, 1)

            def section(ly, at, one, two, tail, query, following=False, handing=None):
                dealt = ly.late if following else ly.first
                finish = dict(zip(FINISH, (reciprocals, normalise, lambda: add_up(ly, at)))) if tail else {}
                if handing:
                    settle(dve, keys_free, 1)
                for slot in range(ly.slots):
                    if following and 1 <= slot <= ly.key_parts:
                        stack_keys(ly, slot - 1, 4 + (slot - 1) % 2)
                        if slot == ly.key_parts:
                            settle(dve, kmasked, ly.key_parts)
                    if following and slot == ly.first_q + 2:
                        hand_queries()
                    if handing:
                        if slot == 2:
                            settle(dve, vals_free, 1)
                        for j in range(ly.pieces):
                            if slot == max(0, 2 * ly.piece * j - 6):
                                hand_over_keys(ly, j)
                            if slot == max(2, 2 * ly.piece * j - 3):
                                hand_over_values(ly, j)
                    if one:
                        pass1(ly, dealt[slot - 1][1] if slot else 0, dealt[slot][1], query)
                    if slot in finish:
                        finish[slot]()
                    if handing and slot == FINISH[3]:
                        hand_over_output(ly, *handing)
                    if following and slot in ly.value_slots:
                        place_values(ly, ly.value_slots[slot], 7)

            def prepare(ly):
                take_weights()
                for i in range(ly.key_parts):
                    stack_keys(ly, i, i % 4)
                settle(dve, kmasked, ly.key_parts)
                for m in range(ly.banks_of_values):
                    place_values(ly, m, 4 + m)
                hand_queries()

            def hand_over_keys(ly, j):
                cols = slice(j * ly.piece * ly.key_rows, (j + 1) * ly.piece * ly.key_rows)
                V.tensor_copy(keys[:, :, cols], keys_one[:, :, cols]).then_inc(keys_handed, 1)

            def hand_over_values(ly, j):
                tiles = slice(j * ly.piece, (j + 1) * ly.piece)
                V.tensor_copy(vals[:, tiles, :, :], vals_next[:, tiles, :, :]).then_inc(vals_handed, 1)

            def hand_over_output(ly, b, g):
                if ly.biased:
                    V.tensor_copy(wout[:, :], wg[:, OW:OW + 128]).then_inc(output_handed, 1)
                else:
                    V.tensor_tensor(wout[:, :], wg[:, OW:OW + 128], pi[:, bass.ds(2 * g + b, 1)].broadcast_to([128, 128]),
                                    ALU.mult).then_inc(output_handed, 1)

            def group(ly, b, after):
                with nc.vector.Fori(1, UNITS - 2) as a:
                    section(ly, b * N + (a - 1) * QB, True, True, True, True)
                more = after is not None
                section(ly, b * N + (UNITS - 3) * QB, True, True, True, False)
                if more:
                    take_weights()
                section(ly, b * N + (UNITS - 2) * QB, more, True, True, more, more)
                if more:
                    section(ly, b * N + (UNITS - 1) * QB, True, True, True, True, handing=(b, after))
                    return
                reciprocals()
                normalise()
                add_up(ly, b * N + (UNITS - 1) * QB)

            def masks(ly):
                V.tensor_scalar(less_q[:, :], cst[:, C_ID:C_ID + 128], cst[:, C_QM + ly.number:C_QM + ly.number + 1],
                                None, ALU.mult)
                V.tensor_scalar(less_k[:, :], cst[:, C_ID:C_ID + 128], cst[:, C_KM + ly.number:C_KM + ly.number + 1],
                                HD ** 0.5, ALU.mult, ALU.mult)

            def pool_source():
                settle(dve, xsrc_loaded, 16)
                img = xsrc[:, :].rearrange("c (y x) -> c y x", x=W)
                px = pooled.rearrange("c (y x) -> c y x", x=HP)
                steps = [
                    lambda: V.tensor_tensor(tall, img[:, :, 0::2], img[:, :, 1::2], ALU.add),
                    lambda: V.tensor_tensor(tall[:, :, 1:HP], tall[:, :, 1:HP], img[:, :, 1:W - 2:2], ALU.add),
                    lambda: V.tensor_tensor(px, tall[:, 0::2, :], tall[:, 1::2, :], ALU.add),
                    lambda: V.tensor_tensor(px[:, 1:HP, :], px[:, 1:HP, :], tall[:, 1:H - 2:2, :], ALU.add),
                    lambda: V.tensor_scalar(pooled, pooled, 1.0 / 9.0, None, ALU.mult),
                    lambda: V.tensor_scalar(px[:, 0, :], px[:, 0, :], 1.5, None, ALU.mult),
                    lambda: V.tensor_scalar(px[:, :, 0], px[:, :, 0], 1.5, None, ALU.mult),
                ]
                for k, step in enumerate(steps):
                    step().then_inc(pool_steps, 1)
                    dve.wait_ge(pool_steps, k + 1)
                settle(dve, pool_steps, len(steps))
                dve.nop(nofuse=True).then_inc(source_ready, 1)

            def layer_norm(b):
                for n in range(UNITS):
                    dve.wait_ge(ln_mean, n + 1)
                    V.tensor_tensor(xsrc[:, n * QB:(n + 1) * QB], xacc[:, bass.ds(b * N + n * QB, QB)], P[:, n, 0:QB],
                                    ALU.subtract).then_inc(ln_cent, 1)
                settle(dve, ln_mean, UNITS)
                for n in range(UNITS):
                    dve.wait_ge(ln_inv, n + 1)
                    cols = slice(n * QB, (n + 1) * QB)
                    last = V.scalar_tensor_tensor(out=xsrc[:, cols], in0=xsrc[:, cols], scalar=sml[:, S_GLN:S_GLN + 1],
                                                  in1=lots[:, n, :], op0=ALU.mult, op1=ALU.mult)
                last.then_inc(source_ready, 1)
                settle(dve, ln_inv, UNITS)

            def layer(ly):
                with nc.vector.Fori(0, NB) as b:
                    if ly.biased:
                        layer_norm(b)
                    else:
                        pool_source()
                    prepare(ly)
                    section(ly, None, True, False, False, True)
                    for j in range(ly.pieces):
                        hand_over_keys(ly, j)
                        hand_over_values(ly, j)
                    hand_over_output(ly, b, 0)
                    section(ly, None, True, True, False, True)
                    with nc.vector.Fori(0, ly.groups - 1) as g:
                        group(ly, b, g + 1)
                    group(ly, b, None)
                    dve.drain().then_inc(group_free, 1)
                    if ly.biased:
                        dve.nop(nofuse=True).then_inc(batch_added, 1)

            masks(L0)
            layer(L0)
            masks(L1)
            V.memset(keys_one[:, :, :], 0.0)
            V.memset(vals_next[:, :, :, :], 0.0).then_inc(vals_cleared, 1)
            dve.wait_ge(vals_cleared, 1)
            V.memset(vals_next[0:W, :, :, HD:HD + 1], 1.0)
            V.memset(vals_next[64:64 + W, :, :, HD:HD + 1], 1.0).then_inc(cleared, 1)
            for s in (*mbias_free, upper_free, lower_free):
                dve.nop(nofuse=True).then_inc(s, 1)
            layer(L1)


def kernel(**inputs):
    import numpy as _np
    import concourse.bacc as _bacc
    from concourse import mybir as _mybir
    from concourse.bass_utils import run_bass_kernel_spmd as _run

    a = {k: _np.asarray(v) for k, v in inputs.items()}
    f = _np.float32

    def pack(wq, bq, wk, bk, wv, bv, wo, groups, heads_of, width, part_of):
        blocks = 48 // width if width == 16 else 4
        w = _np.zeros((groups, 128, WG), f)
        for g in range(groups):
            for s in range(4):
                h, part, p, r = heads_of(g, s), part_of(s), s // 2, s % 2
                rows = slice(h * 16 + part * width, h * 16 + part * width + width)
                for k in range(blocks):
                    at = 64 * r + width * k
                    w[g, :, QW + 128 * p + at:QW + 128 * p + at + width] = wq[rows].T
                    w[g, :, KW + 128 * p + at:KW + 128 * p + at + width] = wk[rows].T
                    w[g, at:at + width, BQ + p] = bq[rows]
                    w[g, at:at + width, BK + p] = bk[rows]
                head = slice(h * 16, h * 16 + 16)
                w[g, :, VW + 16 * s:VW + 16 * s + 16] = wv[head].T
                w[g, 32 * s:32 * s + 16, OW:OW + 128] = wo[:, head].T
                w[g, :, BV + 16 * s:BV + 16 * s + 16] = bv[head]
        return w

    zero = _np.zeros(128, f)
    wq, bq = a['L0_conv_w_qs'], a['L0_conv_b_qs']
    wg0 = pack(wq, bq, wq, bq, a['L0_conv_w_vs'], a['L0_conv_b_vs'], a['L0_conv_w_out'], 4,
               lambda g, s: 2 * g + s // 2, 8, lambda s: s % 2)
    qkv = a['L1_conv_w_qkv']
    wg1 = pack(qkv[0:128], zero, qkv[128:256], zero, qkv[256:384], zero, a['L1_conv_w_out'], 2,
               lambda g, s: 4 * g + s, 16, lambda s: 0)

    small = _np.zeros((128, SW), f)
    mixes = _np.zeros((128, 8, 128), f)
    for j in range(4):
        q = slice(32 * j, 32 * j + 32)
        small[32 * j, S_W0Y + 32 * j:S_W0Y + 32 * j + 32] = a['L1_conv_cpb_w0'][:, 0]
        small[0, S_W0X + 32 * j:S_W0X + 32 * j + 32] = a['L1_conv_cpb_w0'][:, 1]
        small[q, S_W1 + 32 * j:S_W1 + 32 * j + 32] = a['L1_conv_cpb_w1'].T
        small[q, S_W2 + 32 * j:S_W2 + 32 * j + 8] = a['L1_conv_cpb_w2'].T
        small[q, S_B0] = a['L1_conv_cpb_b0']
        small[q, S_B1] = a['L1_conv_cpb_b1']
        small[32 * j:32 * j + 8, S_B2] = a['L1_conv_cpb_b2']
    small[:, S_WQ:S_WQ + 128] = wq.T
    small[:, S_BQ] = bq
    small[:, S_GBN] = a['L0_conv_bn_gamma']
    small[:, S_BETA] = a['L0_conv_bn_beta']
    small[:, S_GLN] = a['L1_conv_gamma'].reshape(128)
    for k in range(2):
        for g in range(4):
            for s in range(4):
                h, m = 2 * g + s // 2, (s % 2) ^ k
                mixes[16 * h:16 * h + 16, 4 * k + g, 32 * s:32 * s + 32] = a['L0_conv_mix_w'][m][:, None]

    consts = _np.zeros((128, CW), f)
    consts[:, C_ID:C_ID + 128] = _np.eye(128, dtype=f)
    for s in range(4):
        consts[32 * s + 16, C_SEL + s] = 1.0
    for half in range(2):
        consts[_np.arange(W) + half * W, C_FLIP + W - 1 - _np.arange(W)] = 1.0
    for r in range(2):
        o = 64 * r
        consts[o + MAXROW, C_ONE] = 1.0
        consts[o + 16:o + 32, C_QM] = -1.0
        consts[o + 32:o + 48, C_QM + 1] = -1.0
        consts[o + 8:o + 16, C_KM] = -1.0
        consts[o + 24:o + 32, C_KM] = -1.0
        consts[o + 16:o + 32, C_KM + 1] = -1.0
    consts[:, C_MEAN:C_MEAN + 128] = 1.0 / 128
    consts[:, C_EPS] = LN_EPS

    arrays = {"in_x": a['x'].reshape(NB, C, N), "in_small": small, "in_mixes": mixes.reshape(128, 1024),
              "in_consts": consts, "in_wg0": wg0, "in_wg1": wg1}
    nc = _bacc.Bacc("TRN2", target_bir_lowering=False, num_devices=1)
    args = [nc.dram_tensor(n, v.shape, _mybir.dt.from_np(v.dtype), kind="ExternalInput").ap() for n, v in arrays.items()]
    args.append(nc.dram_tensor("out_0", (NB, C, N), _mybir.dt.float32, kind="ExternalOutput").ap())
    build(nc, *args)
    r = _run(nc, [arrays], core_ids=[0])
    return r.results[0]["out_0"].reshape(NB, C, H, W)
```
